# Optimizing a Trainium2 kernel written in Bass

```python
import numpy as np
import jax
import jax.numpy as jnp

def _softmax(x, axis=-1):
    return jax.nn.softmax(x, axis=axis)

def _gelu(x):
    return jax.nn.gelu(x, approximate=True)

def _silu(x):
    return jax.nn.silu(x)

def _sigmoid(x):
    return jax.nn.sigmoid(x)

def _layernorm(x, axis=-1, eps=1e-05):
    m = jnp.mean(x, axis=axis, keepdims=True)
    v = jnp.var(x, axis=axis, keepdims=True)
    return (x - m) / jnp.sqrt(v + eps)

def _scatter_add(tgt, idx, src, axis=0):
    return tgt.at[idx].add(src)

def _segment_sum(src, seg, n):
    return jax.ops.segment_sum(src, seg, n)
kernel_name = 'mk_flamingo_gated_d1_seqx_r8_b3ad37'

def setup_inputs(seed: int=0):
    np.random.seed(seed)
    _w = jnp.asarray

    def _rec_inputs():
        import jax
        import jax.numpy as jnp
        _rk = jax.random.key(seed)
        x = 4.136e-05 + 0.9999 * jax.random.normal(jax.random.fold_in(_rk, 1), (4, 256, 256), jnp.float32)
        _lenS = 256 - jax.random.randint(jax.random.fold_in(_rk, 7), (4,), 0, max(1, 256 // 4) + 1, jnp.int32)
        _lenS2 = 256 - jax.random.randint(jax.random.fold_in(_rk, 8), (4,), 0, max(1, 256 // 4) + 1, jnp.int32)
        _ctx_1024P = jax.random.normal(jax.random.fold_in(_rk, 11), (4, 16, 128), jnp.float32)
        _ctx_1024c = jax.random.dirichlet(jax.random.fold_in(_rk, 511), 0.3 * jnp.ones((16,), jnp.float32), (4, 256))
        _ctx_1024t = jnp.einsum('bsk,bkd->bsd', _ctx_1024c, _ctx_1024P)
        _ctx_1024t = _ctx_1024t * jax.lax.rsqrt(jnp.mean(jnp.square(_ctx_1024t)) + 1e-12) * 0.953939
        ctx_1024 = -0.000292821 + 1.00034 * (_ctx_1024t + 0.3 * jax.random.normal(jax.random.fold_in(_rk, 611), (4, 256, 128), jnp.float32))
        _g = jax.random.normal(jax.random.fold_in(_rk, 9001), (2, 1), jnp.float32)
        _g = jnp.sign(_g) * jnp.maximum(jnp.abs(_g), 1.0) + (_g == 0) * 1.0
        g_xattn = _g[0]
        g_ffn = _g[1]
        return (x, ctx_1024, g_xattn, g_ffn)
    x, ctx_1024, g_xattn, g_ffn = _rec_inputs()

    def _L0_xattn_setup():
        import jax, jax.numpy as jnp
        import numpy as np
        import math
        B, L, DM = (2, 256, 128)
        DS, DC, EXP = (16, 4, 2)
        DI = EXP * DM
        DR = math.ceil(DM / 16)
        DT_MIN, DT_MAX, DT_FLOOR = (0.001, 0.1, 0.0001)

        def _ssm_forward(hidden_states, z, in_proj_w, conv_w, conv_b, x_proj_w, dt_proj_w, dt_proj_b, A_log, D):
            b = hidden_states.shape[0]
            x = jnp.einsum('ed,bld->bel', in_proj_w, hidden_states)
            xp = jnp.pad(x, ((0, 0), (0, 0), (DC - 1, 0)))
            xc = jax.lax.conv_general_dilated(xp, conv_w[:, None, :], window_strides=(1,), padding='VALID', dimension_numbers=('NCH', 'OIH', 'NCH'), feature_group_count=DI)
            u = jax.nn.silu(xc + conv_b[None, :, None])
            x_dbl = jnp.einsum('ke,bel->bkl', x_proj_w, u)
            dt_lo = x_dbl[:, :DR]
            Bm = x_dbl[:, DR:DR + DS]
            Cm = x_dbl[:, DR + DS:]
            delta = jax.nn.softplus(jnp.einsum('er,brl->bel', dt_proj_w, dt_lo) + dt_proj_b[None, :, None])
            A = -jnp.exp(A_log)

            def step(state, xs):
                d_t, B_t, C_t, u_t = xs
                dA = jnp.exp(d_t[..., None] * A)
                state = state * dA + (d_t * u_t)[..., None] * B_t[:, None, :]
                y_t = jnp.einsum('ben,bn->be', state, C_t)
                return (state, y_t)
            xs = (jnp.moveaxis(delta, -1, 0), jnp.moveaxis(Bm, -1, 0), jnp.moveaxis(Cm, -1, 0), jnp.moveaxis(u, -1, 0))
            state0 = jnp.zeros((b, DI, DS), delta.dtype)
            _, ys = jax.lax.scan(step, state0, xs)
            y = jnp.moveaxis(ys, 0, -1)
            y = y + D[None, :, None] * u
            y = y * jax.nn.silu(z)
            return jnp.swapaxes(y, 1, 2)
        key = jax.random.key(seed)
        ks = jax.random.split(key, 8)
        hidden_states = jax.random.normal(ks[0], (B, L, DM), jnp.float32)
        z = jax.random.normal(ks[1], (B, DI, L), jnp.float32)
        in_proj_w = jax.random.normal(ks[2], (DI, DM), jnp.float32) * DM ** (-0.5)
        conv_w = jax.random.normal(ks[3], (DI, DC), jnp.float32) * DC ** (-0.5)
        conv_b = jnp.zeros((DI,), jnp.float32)
        x_proj_w = jax.random.normal(ks[4], (DR + 2 * DS, DI), jnp.float32) * DI ** (-0.5)
        dt_std = DR ** (-0.5)
        dt_proj_w = jax.random.uniform(ks[5], (DI, DR), jnp.float32, -dt_std, dt_std)
        dt = jnp.exp(jax.random.uniform(ks[6], (DI,), jnp.float32) * (math.log(DT_MAX) - math.log(DT_MIN)) + math.log(DT_MIN))
        dt = jnp.clip(dt, DT_FLOOR)
        dt_proj_b = dt + jnp.log(-jnp.expm1(-dt))
        A_log = jnp.log(jnp.broadcast_to(jnp.arange(1, DS + 1, dtype=jnp.float32), (DI, DS)))
        D = jnp.ones((DI,), jnp.float32)
        return dict(hidden_states=hidden_states, z=z, in_proj_w=in_proj_w, conv_w=conv_w, conv_b=conv_b, x_proj_w=x_proj_w, dt_proj_w=dt_proj_w, dt_proj_b=dt_proj_b, A_log=A_log, D=D)
    _L0_xattn_all = _L0_xattn_setup()
    _L0_xattn_in = {k: v for k, v in _L0_xattn_all.items() if k in ('in_proj_w', 'conv_w', 'conv_b', 'x_proj_w', 'dt_proj_w', 'dt_proj_b', 'A_log', 'D')}
    del _L0_xattn_all

    def _L0_ffn_setup():
        import jax, jax.numpy as jnp
        import numpy as np
        HIDDEN = 256
        N_EXPERTS = 8
        N_SHARED = 2
        TOP_K = 2
        MOE_FF = 176
        SHARED_FF = N_SHARED * MOE_FF
        SCALE = 2.5
        BATCH, SEQ = (2, 128)
        key = jax.random.key(seed)
        ks = jax.random.split(key, 8)
        s = 0.02
        return {'hidden_states': jax.random.normal(ks[0], (BATCH, SEQ, HIDDEN), jnp.float32), 'gate_w': jax.random.normal(ks[1], (N_EXPERTS, HIDDEN), jnp.float32) * s, 'shared_wg': jax.random.normal(ks[2], (SHARED_FF, HIDDEN), jnp.float32) * s, 'shared_wu': jax.random.normal(ks[3], (SHARED_FF, HIDDEN), jnp.float32) * s, 'shared_wd': jax.random.normal(ks[4], (HIDDEN, SHARED_FF), jnp.float32) * s, 'exp_wg': jax.random.normal(ks[5], (N_EXPERTS, MOE_FF, HIDDEN), jnp.float32) * s, 'exp_wu': jax.random.normal(ks[6], (N_EXPERTS, MOE_FF, HIDDEN), jnp.float32) * s, 'exp_wd': jax.random.normal(ks[7], (N_EXPERTS, HIDDEN, MOE_FF), jnp.float32) * s}
    _L0_ffn_all = _L0_ffn_setup()
    _L0_ffn_in = {k: v for k, v in _L0_ffn_all.items() if k in ('gate_w', 'shared_wg', 'shared_wu', 'shared_wd', 'exp_wg', 'exp_wu', 'exp_wd')}
    del _L0_ffn_all
    return {'x': x, 'ctx_1024': ctx_1024, 'g_xattn': g_xattn, 'g_ffn': g_ffn, 'L0_xattn_in_proj_w': _L0_xattn_in['in_proj_w'], 'L0_xattn_conv_w': _L0_xattn_in['conv_w'], 'L0_xattn_conv_b': _L0_xattn_in['conv_b'], 'L0_xattn_x_proj_w': _L0_xattn_in['x_proj_w'], 'L0_xattn_dt_proj_w': _L0_xattn_in['dt_proj_w'], 'L0_xattn_dt_proj_b': _L0_xattn_in['dt_proj_b'], 'L0_xattn_A_log': _L0_xattn_in['A_log'], 'L0_xattn_D': _L0_xattn_in['D'], 'L0_ffn_gate_w': _L0_ffn_in['gate_w'], 'L0_ffn_shared_wg': _L0_ffn_in['shared_wg'], 'L0_ffn_shared_wu': _L0_ffn_in['shared_wu'], 'L0_ffn_shared_wd': _L0_ffn_in['shared_wd'], 'L0_ffn_exp_wg': _L0_ffn_in['exp_wg'], 'L0_ffn_exp_wu': _L0_ffn_in['exp_wu'], 'L0_ffn_exp_wd': _L0_ffn_in['exp_wd']}

def reference(x, ctx_1024, g_xattn, g_ffn, L0_xattn_in_proj_w, L0_xattn_conv_w, L0_xattn_conv_b, L0_xattn_x_proj_w, L0_xattn_dt_proj_w, L0_xattn_dt_proj_b, L0_xattn_A_log, L0_xattn_D, L0_ffn_gate_w, L0_ffn_shared_wg, L0_ffn_shared_wu, L0_ffn_shared_wd, L0_ffn_exp_wg, L0_ffn_exp_wu, L0_ffn_exp_wd):
    import jax
    import jax.numpy as jnp

    def _L0_xattn_ref(hidden_states, z, in_proj_w, conv_w, conv_b, x_proj_w, dt_proj_w, dt_proj_b, A_log, D):
        import jax, jax.numpy as jnp
        import numpy as np
        import math
        B, L, DM = (2, 256, 128)
        DS, DC, EXP = (16, 4, 2)
        DI = EXP * DM
        DR = math.ceil(DM / 16)
        DT_MIN, DT_MAX, DT_FLOOR = (0.001, 0.1, 0.0001)

        def _ssm_forward(hidden_states, z, in_proj_w, conv_w, conv_b, x_proj_w, dt_proj_w, dt_proj_b, A_log, D):
            b = hidden_states.shape[0]
            x = jnp.einsum('ed,bld->bel', in_proj_w, hidden_states)
            xp = jnp.pad(x, ((0, 0), (0, 0), (DC - 1, 0)))
            xc = jax.lax.conv_general_dilated(xp, conv_w[:, None, :], window_strides=(1,), padding='VALID', dimension_numbers=('NCH', 'OIH', 'NCH'), feature_group_count=DI)
            u = jax.nn.silu(xc + conv_b[None, :, None])
            x_dbl = jnp.einsum('ke,bel->bkl', x_proj_w, u)
            dt_lo = x_dbl[:, :DR]
            Bm = x_dbl[:, DR:DR + DS]
            Cm = x_dbl[:, DR + DS:]
            delta = jax.nn.softplus(jnp.einsum('er,brl->bel', dt_proj_w, dt_lo) + dt_proj_b[None, :, None])
            A = -jnp.exp(A_log)

            def step(state, xs):
                d_t, B_t, C_t, u_t = xs
                dA = jnp.exp(d_t[..., None] * A)
                state = state * dA + (d_t * u_t)[..., None] * B_t[:, None, :]
                y_t = jnp.einsum('ben,bn->be', state, C_t)
                return (state, y_t)
            xs = (jnp.moveaxis(delta, -1, 0), jnp.moveaxis(Bm, -1, 0), jnp.moveaxis(Cm, -1, 0), jnp.moveaxis(u, -1, 0))
            state0 = jnp.zeros((b, DI, DS), delta.dtype)
            _, ys = jax.lax.scan(step, state0, xs)
            y = jnp.moveaxis(ys, 0, -1)
            y = y + D[None, :, None] * u
            y = y * jax.nn.silu(z)
            return jnp.swapaxes(y, 1, 2)
        return _ssm_forward(hidden_states, z, in_proj_w, conv_w, conv_b, x_proj_w, dt_proj_w, dt_proj_b, A_log, D)

    def _L0_ffn_ref(hidden_states, gate_w, shared_wg, shared_wu, shared_wd, exp_wg, exp_wu, exp_wd):
        import jax, jax.numpy as jnp
        import numpy as np
        HIDDEN = 256
        N_EXPERTS = 8
        N_SHARED = 2
        TOP_K = 2
        MOE_FF = 176
        SHARED_FF = N_SHARED * MOE_FF
        SCALE = 2.5
        BATCH, SEQ = (2, 128)
        B, S, D = hidden_states.shape
        T = B * S
        xf = hidden_states.reshape(T, D)
        scores = jax.nn.sigmoid(xf @ gate_w.T)
        topk_w, topk_idx = jax.lax.top_k(scores, TOP_K)
        topk_w = topk_w / (topk_w.sum(axis=-1, keepdims=True) + 1e-20)
        topk_w = topk_w * SCALE
        shared_out = jax.nn.silu(xf @ shared_wg.T) * (xf @ shared_wu.T) @ shared_wd.T
        h = jax.nn.silu(jnp.einsum('td,efd->etf', xf, exp_wg)) * jnp.einsum('td,efd->etf', xf, exp_wu)
        all_out = jnp.einsum('etf,edf->etd', h, exp_wd)
        picked = all_out[topk_idx, jnp.arange(T)[:, None]]
        routed_out = (topk_w[..., None] * picked).sum(axis=1)
        return (shared_out + routed_out).reshape(B, S, D)
    x = x + jnp.tanh(g_xattn[0]) * _L0_xattn_ref(ctx_1024, _layernorm(x, axis=-1), L0_xattn_in_proj_w, L0_xattn_conv_w, L0_xattn_conv_b, L0_xattn_x_proj_w, L0_xattn_dt_proj_w, L0_xattn_dt_proj_b, L0_xattn_A_log, L0_xattn_D)
    x = x + jnp.tanh(g_ffn[0]) * _L0_ffn_ref(_layernorm(x, axis=-1), L0_ffn_gate_w, L0_ffn_shared_wg, L0_ffn_shared_wu, L0_ffn_shared_wd, L0_ffn_exp_wg, L0_ffn_exp_wu, L0_ffn_exp_wd)
    return x

_drawn_inputs = setup_inputs


def setup_inputs(seed=0):
    import zlib

    import numpy as np

    out = dict(_drawn_inputs(seed))
    spreads = {'L0_xattn_conv_b': (0.0, 0.1), 'L0_xattn_D': (1.0, 0.2)}
    factors = {'L0_xattn_dt_proj_w': 7.761,
     'L0_xattn_dt_proj_b': 3.267,
     'L0_xattn_A_log': 2.875,
     'L0_ffn_gate_w': 9.898,
     'L0_ffn_shared_wg': 3.156,
     'L0_ffn_shared_wu': 3.111,
     'L0_ffn_shared_wd': 3.111,
     'L0_ffn_exp_wg': 2.993,
     'L0_ffn_exp_wu': 2.967,
     'L0_ffn_exp_wd': 2.953}
    for name, (base, spread) in spreads.items():
        noise = np.random.default_rng([zlib.crc32(name.encode()), seed]).standard_normal(out[name].shape)
        drawn = base * np.exp(spread * noise) if base else spread * noise
        out[name] = jnp.asarray(drawn.astype(out[name].dtype))
    for name, factor in factors.items():
        out[name] = (out[name] * factor).astype(out[name].dtype)
    return out
```

```python
from contextlib import ExitStack

import numpy as np

import concourse.bass as bass
from concourse import mybir

F32 = mybir.dt.float32
BF16 = mybir.dt.bfloat16
U32 = mybir.dt.uint32
ALU = mybir.AluOpType
ACT = mybir.ActivationFunctionType

P = 128
B, L, D = 4, 256, 256
DM, DI, DS, DC, DR = 128, 256, 16, 4, 8
EH = DI // P
LH = L // P
KT = D // P
NE, FF = 8, 176
NU = NE + 2
FCAT = NU * FF
FB = (FCAT + P - 1) // P
LASTF = FCAT - (FB - 1) * P
SCALE = 2.5
EPS = 1e-5

PC_CONVW = 0
PC_CONVB = PC_CONVW + EH * DC
PC_DTB = PC_CONVB + EH
PC_D = PC_DTB + EH
PC_ALOG = PC_D + EH
PC_GX = PC_ALOG + EH * DS
PC_GF = PC_GX + 1
PC_IOTA = PC_GF + 1
NPC = PC_IOTA + NE

XROWS = 3 * 2 * DS
XM = XROWS + DR

DA_RING, DBU_RING, PROD_RING, BB_RING, HT_RING = 2, 3, 3, 4, 3

UNITS = B * LH * NU
GROUPS = [(0, 4), (4, 8), (8, 12), (12, FB)]
NG = len(GROUPS)


def group_last_unit(g):
    return (min(GROUPS[g][1] * P, FCAT) - 1) // FF


def schedule():
    order = [("load", 0)]
    order += [(t, 0) for t in ("project", "conv", "silu_u", "xproj", "split", "dt", "softplus", "delta")]
    order += [("spread_b", 0), ("first", 0)]
    steps = B * DS
    before = {6: (["project"], ["conv"]), 7: ([], ["silu_u"]), 8: (["xproj"], ["split"]), 9: (["dt"], ["softplus"]),
              11: ([], ["delta"])}
    behind = {1: ([], ["gate_y"]), 2: (["to_tokens"], ["residual"]), 3: ([], ["norm"]), 4: (["to_features"], []),
              5: (["logits"], ["route"])}
    z = {0: ["z_stats"], 12: ["z_norm"], 14: ["z_gate"]}
    unit_at = {}
    for u in range(UNITS):
        b, j = divmod(u, LH * NU)
        unit_at.setdefault(DS * (b + 1) + 5 + j * DS // (LH * NU), []).append(u)
    for s in range(DS * (B + 1) + 5 + DS):
        b, n = divmod(s, DS)
        units = unit_at.get(s, [])
        if units:
            order += [("up", units[0]), ("gate", units[0])]
        if s % 2 == 0 and s + 2 < steps:
            order.append(("spread_b", s // 2 + 1))
        fill, follow = [], []
        if b + 1 < B and n in before:
            fill += [(t, b + 1) for t in before[n][0]]
            follow += [(t, b + 1) for t in before[n][1]]
        if 1 <= b <= B and n in behind:
            fill += [(t, b - 1) for t in behind[n][0]]
            follow += [(t, b - 1) for t in behind[n][1]]
        if b < B and n in z:
            follow += [(t, b) for t in z[n]]
        order += fill
        if s < steps:
            order.append(("scan", s))
        if units:
            order.append(("mul", units[0]))
        order += follow
        if 1 <= s <= steps:
            order.append(("prod", s - 1))
        for u in units[1:]:
            order += [("up", u), ("gate", u), ("mul", u)]
    return order + [("flush", UNITS)]


def mixer(nc, ctxT, x, params, w_in, w_x, w_dt, w_gate, w_up, w_down, ident_in, sel_in, out):
    order = schedule()
    with ExitStack() as stack:
        def sb(name, shape, dt=F32):
            return stack.enter_context(nc.sbuf_tensor(name, shape, dt))

        def ps(name, shape, dt=F32):
            return stack.enter_context(nc.psum_tensor(name, shape, dt))

        def sem(name):
            return stack.enter_context(nc.semaphore(name))

        ctx_sb = sb("ctx_sb", [P, B, L])
        x_sb = sb("x_sb", [P, B, LH, D])
        par = sb("par", [P, NPC])
        win = sb("win", [P, DI])
        wx = sb("wx", [P, EH, XM])
        wdt = sb("wdt", [P, DI])
        wg = sb("wg", [P, KT, NE])
        wup = sb("wup", [P, KT, NU, 2 * FF])
        wdn = sb("wdn", [P, FB, D])
        ident = sb("ident", [P, P])
        sel = sb("sel", [P, 2 * DS, P], BF16)
        cwh = sb("cwh", [P, EH * DC + EH])
        aneg = sb("aneg", [P, EH * DS])
        aexp = sb("aexp", [P, EH * DS])
        gtanh = sb("gtanh", [P, 2])
        gates = sb("gates", [P, 2])
        minus_half = sb("minus_half", [P, B * LH])
        zst = sb("zst", [P, B * LH, 6])
        zmv = sb("zmv", [P, B * LH, 2])
        zve = sb("zve", [P, B * LH])
        zrs = sb("zrs", [P, B * LH])
        zn = sb("zn", [P, LH, L])
        zt = sb("zt", [P, LH, L])
        sz = sb("sz", [P, 2, LH, L])
        xh = sb("xh", [P, 2, EH, L])
        tu = sb("tu", [P, EH, L])
        u = sb("u", [P, 2, EH, L])
        dtlo = sb("dtlo", [P, L])
        parts = sb("parts", [XROWS, 2, L], BF16)
        rest1 = sb("rest1", [2 * 2 * DS, L])
        rest2 = sb("rest2", [2 * DS, L])
        dabs = sb("dabs", [P, EH, L])
        dexp = sb("dexp", [P, EH, L])
        dln = sb("dln", [P, EH, L])
        drel = sb("drel", [P, EH, L])
        dy = sb("dy", [P, EH, L])
        dnc = sb("dnc", [P, EH, L])
        dsum = sb("dsum", [P, EH, L])
        delta = sb("delta", [P, 2, EH, L])
        du = sb("du", [P, 2, EH, L])
        uD = sb("uD", [P, 2, EH, L])
        bb = sb("bb", [P, BB_RING, 2, L])
        dbu = sb("dbu", [P, DBU_RING, EH, L])
        hs = sb("hs", [P, 2, EH, L])
        prod = sb("prod", [P, PROD_RING, EH, L])
        acc = sb("acc", [P, 2, EH, L])
        ysum = sb("ysum", [P, EH, L])
        yg = sb("yg", [P, EH, L])
        x2 = sb("x2", [P, B, LH, D])
        st2 = sb("st2", [P, LH, 6])
        mv2 = sb("mv2", [P, LH, 2])
        ve2 = sb("ve2", [P, LH])
        rs2 = sb("rs2", [P, LH])
        hn = sb("hn", [P, LH, D])
        hnT = sb("hnT", [P, 2, KT, L])
        rex = sb("rex", [P, LH * NE])
        rs1 = sb("rs1", [P, LH * NE])
        score = sb("score", [P, LH * NE])
        top = sb("top", [P, LH, 8])
        topi = sb("topi", [P, LH, 8], U32)
        topf = sb("topf", [P, LH, 2])
        den = sb("den", [P, LH])
        rden = sb("rden", [P, LH])
        topw = sb("topw", [P, LH, 2])
        pick = sb("pick", [P, LH, 2, NE])
        wtok = sb("wtok", [P, 2, LH, NE])
        tg = sb("tg", [P, 2, FF])
        ag = sb("ag", [P, 2, FF])
        hcat = sb("hcat", [P, 2, FCAT])
        hT = sb("hT", [P, HT_RING, 4 * P])
        outb = sb("outb", [P, 2, D])

        psA = ps("psA", [P, DA_RING, EH, L])
        psC = ps("psC", [P, 2, 512])
        psM = ps("psM", [P, 512])
        psU = ps("psU", [P, 2, 512])
        psD = ps("psD", [P, 2, D])

        d_par, d_ctx0, d_ctx, d_win, d_wx = sem("d_par"), sem("d_ctx0"), sem("d_ctx"), sem("d_win"), sem("d_wx")
        d_wdt, d_id, d_sel, d_x0, d_x = sem("d_wdt"), sem("d_id"), sem("d_sel"), sem("d_x0"), sem("d_x")
        d_wg, d_wup, d_wdn = sem("d_wg"), sem("d_wup"), sem("d_wdn")
        d_out = [sem("d_out0"), sem("d_out1")]
        s_half, s_aexp, s_aneg, s_gt, s_gates = sem("s_half"), sem("s_aexp"), sem("s_aneg"), sem("s_gt"), sem("s_gates")
        s_mh, s_zero = sem("s_mh"), sem("s_zero")
        s_zst, s_zmv, s_zve, s_zrs, s_zn, s_zt, s_sz = (sem("s_zst"), sem("s_zmv"), sem("s_zve"), sem("s_zrs"),
                                                       sem("s_zn"), sem("s_zt"), sem("s_sz"))
        s_xin, s_xh, s_tap, s_tu, s_u = sem("s_xin"), sem("s_xh"), sem("s_tap"), sem("s_tu"), sem("s_u")
        s_xdbl, s_dtlo, s_hi, s_rest, s_parts = sem("s_xdbl"), sem("s_dtlo"), sem("s_hi"), sem("s_rest"), sem("s_parts")
        s_dtp, s_soft, s_del, s_delta, s_du, s_uD = (sem("s_dtp"), sem("s_soft"), sem("s_del"), sem("s_delta"),
                                                    sem("s_du"), sem("s_uD"))
        s_bps, s_bb, s_cps, s_dA, s_dbu = sem("s_bps"), sem("s_bb"), sem("s_cps"), sem("s_dA"), sem("s_dbu")
        s_scan, s_prod, s_add, s_nsum = sem("s_scan"), sem("s_prod"), sem("s_add"), sem("s_nsum")
        s_ys, s_yg, s_yT, s_x2, s_st2, s_mv2, s_ve2, s_rs2 = (sem("s_ys"), sem("s_yg"), sem("s_yT"), sem("s_x2"),
                                                             sem("s_st2"), sem("s_mv2"), sem("s_ve2"), sem("s_rs2"))
        s_hn, s_hT2, s_hnT, s_log, s_rex, s_rt, s_w = (sem("s_hn"), sem("s_hT2"), sem("s_hnT"), sem("s_log"),
                                                       sem("s_rex"), sem("s_rt"), sem("s_w"))
        s_up, s_tanh, s_ag, s_mul, s_tr, s_ht, s_dn, s_fin = (sem("s_up"), sem("s_tanh"), sem("s_ag"), sem("s_mul"),
                                                             sem("s_tr"), sem("s_ht"), sem("s_dn"), sem("s_fin"))
        s_chain = sem("s_chain")

        Wh = cwh[:, 0:EH * DC].rearrange("p (h k) -> p h k", h=EH)

        def wide(ap, n):
            return ap.unsqueeze(1).broadcast_to([ap.shape[0], n, ap.shape[1]])

        def groups_after(unit, lag):
            u0 = unit - lag
            if u0 < 0 or u0 >= UNITS:
                return []
            t, j = divmod(u0, NU)
            return [NG * t + g for g in range(NG) if group_last_unit(g) == j]

        block = stack.enter_context(nc.Block())

        @block.sync
        def _(sp):
            sp.dma_start(ctx_sb[:, 0, :], ctxT[:, 0, :]).then_inc(d_ctx0, 16)
            sp.dma_start(wx[:, :, :], w_x).then_inc(d_wx, 16)
            sp.dma_start(sel[0:XROWS, :, :], sel_in).then_inc(d_sel, 16)
            sp.dma_start(x_sb[:, 0], x[0].rearrange("(h p) d -> p h d", p=P)).then_inc(d_x0, 16)
            sp.dma_start(ctx_sb[:, 1:B, :], ctxT[:, 1:B, :]).then_inc(d_ctx, 16)
            for b in range(1, B):
                sp.dma_start(x_sb[:, b], x[b].rearrange("(h p) d -> p h d", p=P)).then_inc(d_x, 16)
            sp.dma_start(wg[:, :, :], w_gate).then_inc(d_wg, 16)
            for k in range(KT):
                sp.dma_start(wup[:, k], w_up[:, k]).then_inc(d_wup, 16)
            sp.dma_start(wdn[:, 0:FB - 1, :], w_down[0:(FB - 1) * P].rearrange("(f p) d -> p f d", p=P)).then_inc(d_wdn, 16)
            sp.dma_start(wdn[0:LASTF, FB - 1, :], w_down[(FB - 1) * P:FCAT]).then_inc(d_wdn, 16)
            for t in range(B * LH):
                b, h = divmod(t, LH)
                sp.wait_ge(s_fin, t + 1)
                sp.dma_start(out[b, h * P:(h + 1) * P, :], outb[:, t % 2, :]).then_inc(d_out[t % 2], 16)
            for q in d_out:
                sp.wait_ge(q, 16 * B * LH // 2)

        @block.tensor
        def _(pe):
            psM_read = []

            def take_misc(reader, value):
                if psM_read:
                    pe.wait_ge(*psM_read.pop())
                psM_read.append((reader, value))

            def spread_b(k):
                b = 2 * k // DS
                take_misc(s_bb, k + 1)
                pe.wait_ge(s_parts, b + 1)
                for i in range(2):
                    last = pe.matmul(psM[:, i * L:(i + 1) * L], sel[0:XROWS, (2 * k + i) % DS, :], parts[:, b % 2, :],
                                     start=True, stop=True)
                last.then_inc(s_bps, 1)

            for task, i in order:
                if task == "project":
                    take_misc(s_tap, EH * (DC - 1) * (i + 1))
                    if i == 0:
                        pe.wait_ge(d_ctx0, 16)
                        pe.wait_ge(d_win, 16)
                    if i == 1:
                        pe.wait_ge(d_ctx, 16)
                    for h in range(EH):
                        last = pe.matmul(psM[:, h * L:(h + 1) * L], win[:, h * P:(h + 1) * P], ctx_sb[:, i, :],
                                         start=True, stop=True)
                    last.then_inc(s_xin, 1)
                elif task == "xproj":
                    take_misc(s_rest, i + 1)
                    if i == 0:
                        pe.wait_ge(d_wx, 16)
                    pe.wait_ge(s_u, i + 1)
                    for h in range(EH):
                        last = pe.matmul(psM[0:XM, 0:L], wx[:, h, :], u[:, i % 2, h, :], start=(h == 0), stop=(h == EH - 1))
                    last.then_inc(s_xdbl, 1)
                elif task == "dt":
                    take_misc(s_soft, 6 * i + 4)
                    if i == 0:
                        pe.wait_ge(d_wdt, 16)
                    pe.wait_ge(s_dtlo, i + 1)
                    for h in range(EH):
                        last = pe.matmul(psM[:, h * L:(h + 1) * L], wdt[XROWS:XM, h * P:(h + 1) * P],
                                         dtlo[XROWS:XM, :], start=True, stop=True)
                    last.then_inc(s_dtp, 1)
                elif task == "spread_b":
                    if i == 0:
                        pe.wait_ge(d_sel, 16)
                    spread_b(i)
                elif task == "scan":
                    b, n = divmod(i, DS)
                    if i >= 2:
                        pe.wait_ge(s_prod, i - 1)
                    pe.matmul(psC[:, i % 2, 0:L], sel[0:XROWS, DS + n, :], parts[:, b % 2, :],
                              start=True, stop=True).then_inc(s_cps, 1)
                elif task == "prod" and i < DS:
                    if i == 0:
                        pe.wait_ge(d_id, 16)
                    pe.wait_ge(s_prod, i + 1)
                    pe.matmul(psD[:, :, :], ident[:, :], prod[:, i % PROD_RING], start=(i == 0),
                              stop=(i == DS - 1)).then_inc(s_nsum, 1)
                elif task == "to_tokens":
                    take_misc(s_x2, i + 1)
                    pe.wait_ge(s_yg, i + 1)
                    for lh in range(LH):
                        for h in range(EH):
                            last = pe.transpose(psM[:, lh * D + h * P:lh * D + (h + 1) * P],
                                                yg[:, h, lh * P:(lh + 1) * P], ident[:, :])
                    last.then_inc(s_yT, 1)
                elif task == "to_features":
                    take_misc(s_hnT, i + 1)
                    pe.wait_ge(s_hn, LH * (i + 1))
                    for k in range(KT):
                        for lh in range(LH):
                            last = pe.transpose(psM[:, k * L + lh * P:k * L + (lh + 1) * P],
                                                hn[:, lh, k * P:(k + 1) * P], ident[:, :])
                    last.then_inc(s_hT2, 1)
                elif task == "logits":
                    take_misc(s_rex, i + 1)
                    if i == 0:
                        pe.wait_ge(d_wg, 16)
                    pe.wait_ge(s_hnT, i + 1)
                    for lh in range(LH):
                        for k in range(KT):
                            last = pe.matmul(psM[:, lh * NE:(lh + 1) * NE], hnT[:, i % 2, k, lh * P:(lh + 1) * P],
                                             wg[:, k, :], start=(k == 0), stop=(k == KT - 1))
                    last.then_inc(s_log, 1)
                if task in ("up", "flush"):
                    for unit in ([i] if task == "up" else range(UNITS, UNITS + 4)):
                        if unit < UNITS:
                            t, j = divmod(unit, NU)
                            b, lh = divmod(t, LH)
                            if unit == 0:
                                pe.wait_ge(d_wup, 16 * KT)
                            pe.wait_ge(s_hnT, b + 1)
                            if unit >= 2:
                                pe.wait_ge(s_mul, unit - 1)
                            for k in range(KT):
                                last = pe.matmul(psU[:, unit % 2, 0:2 * FF], hnT[:, b % 2, k, lh * P:(lh + 1) * P],
                                                 wup[:, k, j, :], start=(k == 0), stop=(k == KT - 1))
                            last.then_inc(s_up, 1)
                        for g in groups_after(unit, 2):
                            t, q = divmod(g, NG)
                            take_misc(s_ht, g + 1)
                            pe.wait_ge(s_mul, unit - 1)
                            for f in range(*GROUPS[q]):
                                m = P if f < FB - 1 else LASTF
                                c = (f - GROUPS[q][0]) * P
                                last = pe.transpose(psM[0:m, c:c + P], hcat[:, t % 2, f * P:f * P + m], ident[:, :])
                            last.then_inc(s_tr, 1)
                        for g in groups_after(unit, 3):
                            t, q = divmod(g, NG)
                            if g == 0:
                                pe.wait_ge(d_wdn, 32)
                            if q == 0 and t >= 1:
                                pe.wait_ge(s_fin, t)
                            if q == 0 and t == 0:
                                pe.wait_ge(s_ys, 1)
                            pe.wait_ge(s_ht, g + 1)
                            for f in range(*GROUPS[q]):
                                m = P if f < FB - 1 else LASTF
                                c = (f - GROUPS[q][0]) * P
                                last = pe.matmul(psD[:, 0, :], hT[0:m, g % HT_RING, c:c + P], wdn[0:m, f, :],
                                                 start=(f == 0), stop=(f == FB - 1))
                            last.then_inc(s_dn, 1)

        @block.scalar
        def _(act):
            act.dma_start(par[:, :], params).then_inc(d_par, 16)
            act.dma_start(win[:, :], w_in).then_inc(d_win, 16)
            act.dma_start(wdt[XROWS:XM, :], w_dt).then_inc(d_wdt, 16)
            act.dma_start(ident[:, :], ident_in).then_inc(d_id, 16)

            def exps(m):
                b, n = divmod(m, DS)
                if n == 0:
                    act.wait_ge(s_delta, b + 1)
                if m == 0:
                    act.wait_ge(s_aneg, 1)
                    act.wait_ge(s_zero, 1)
                if m >= DA_RING:
                    act.wait_ge(s_scan, m - DA_RING + 1)
                for h in range(EH):
                    last = act.activation(psA[:, m % DA_RING, h, 1:L], delta[:, b % 2, h, 1:L], ACT.Exp,
                                          scale=aneg[:, h * DS + n:h * DS + n + 1])
                last.then_inc(s_dA, 1)

            def copy_b(k):
                act.wait_ge(s_bps, k + 1)
                if k >= BB_RING:
                    act.wait_ge(s_dbu, 2 * (k - BB_RING) + 2)
                act.copy(bb[:, k % BB_RING].rearrange("p s l -> p (s l)"), psM[:, :]).then_inc(s_bb, 1)

            for task, i in order:
                if task == "load":
                    act.wait_ge(d_par, 16)
                    act.activation(gtanh[:, :], par[:, PC_GX:PC_GX + 2], ACT.Tanh).then_inc(s_gt, 1)
                    act.activation(aexp[:, :], par[:, PC_ALOG:PC_ALOG + EH * DS], ACT.Exp).then_inc(s_aexp, 1)
                elif task == "project":
                    act.wait_ge(s_xin, i + 1)
                    if i == 0:
                        act.wait_ge(s_half, 1)
                    if i >= 2:
                        act.wait_ge(s_u, i - 1)
                    for h in range(EH):
                        act.activation(xh[:, i % 2, h, :], psM[:, h * L:(h + 1) * L], ACT.Identity,
                                       scale=Wh[:, h, DC - 1:DC],
                                       bias=cwh[:, EH * DC + h:EH * DC + h + 1]).then_inc(s_xh, 1)
                elif task == "silu_u":
                    act.wait_ge(s_tap, EH * (DC - 1) * (i + 1))
                    if i >= 1:
                        act.wait_ge(s_u, i)
                    act.activation(tu[:, :, :], xh[:, i % 2], ACT.Tanh).then_inc(s_tu, 1)
                elif task == "xproj":
                    act.wait_ge(s_xdbl, i + 1)
                    if i >= 1:
                        act.wait_ge(s_dtp, i)
                    act.copy(dtlo[XROWS:XM, :], psM[XROWS:XM, 0:L]).then_inc(s_dtlo, 1)
                    if i >= 2:
                        act.wait_ge(s_cps, DS * (i - 1))
                        act.wait_ge(s_bps, DS * (i - 1) // 2)
                    act.copy(parts[:, i % 2, :], psM[0:XROWS, 0:L]).then_inc(s_hi, 1)
                elif task == "softplus":
                    act.preload_act_table_set("natural_log_exp_and_others")
                    act.wait_ge(s_dtp, i + 1)
                    if i >= 1:
                        act.wait_ge(s_delta, i)
                    for h in range(EH):
                        act.activation(dabs[:, h, :], psM[:, h * L:(h + 1) * L], ACT.Abs,
                                       bias=par[:, PC_DTB + h:PC_DTB + h + 1]).then_inc(s_soft, 1)
                    for h in range(EH):
                        last = act.activation(drel[:, h, :], psM[:, h * L:(h + 1) * L], ACT.Relu,
                                              bias=par[:, PC_DTB + h:PC_DTB + h + 1])
                        last.then_inc(s_soft, 1)
                    act.wait_ge(s_soft, 6 * i + 2)
                    act.activation(dexp[:, :, :], dabs[:, :, :], ACT.Exp, scale=-1.0).then_inc(s_soft, 1)
                    act.wait_ge(s_soft, 6 * i + 5)
                    act.activation(dln[:, :, :], dexp[:, :, :], ACT.Ln, bias=1.0).then_inc(s_soft, 1)
                    if i >= 2:
                        act.wait_ge(s_add if i > 2 else s_ys, DS * (i - 2) + 1 - DS if i > 2 else 1)
                    for h in range(EH):
                        act.activation(uD[:, i % 2, h, :], u[:, i % 2, h, :], ACT.Copy,
                                       scale=par[:, PC_D + h:PC_D + h + 1]).then_inc(s_uD, 1)
                elif task == "spread_b":
                    copy_b(i)
                elif task == "first":
                    exps(0)
                elif task == "scan":
                    if i + 1 < B * DS:
                        exps(i + 1)
                elif task == "z_gate":
                    act.wait_ge(s_zn, LH * (i + 1))
                    if i >= 1:
                        act.wait_ge(s_sz, i)
                    act.activation(zt[:, :, :], zn[:, :, :], ACT.Tanh, scale=0.5).then_inc(s_zt, 1)
                elif task == "to_features":
                    act.wait_ge(s_hT2, i + 1)
                    if i >= 2:
                        act.wait_ge(s_up, LH * NU * (i - 1))
                    act.copy(hnT[:, i % 2, :, :].rearrange("p k l -> p (k l)"), psM[:, :]).then_inc(s_hnT, 1)
                elif task == "logits":
                    act.wait_ge(s_log, i + 1)
                    if i >= 1:
                        act.wait_ge(s_w, i)
                    act.activation(rex[:, :], psM[:, 0:LH * NE], ACT.Exp, scale=-1.0).then_inc(s_rex, 1)
                if task in ("up", "flush"):
                    for unit in ([i] if task == "up" else range(UNITS, UNITS + 4)):
                        if unit < UNITS:
                            act.wait_ge(s_up, unit + 1)
                            if unit >= 2:
                                act.wait_ge(s_ag, unit - 1)
                            act.activation(tg[:, unit % 2, :], psU[:, unit % 2, 0:FF], ACT.Tanh,
                                           scale=0.5).then_inc(s_tanh, 1)
                        for g in groups_after(unit, 2):
                            q = g % NG
                            act.wait_ge(s_tr, g + 1)
                            if g >= HT_RING:
                                act.wait_ge(s_dn, g - HT_RING + 1)
                            full = sum(1 for f in range(*GROUPS[q]) if f < FB - 1) * P
                            last = act.copy(hT[:, g % HT_RING, 0:full], psM[:, 0:full])
                            if q == NG - 1:
                                last = act.copy(hT[0:LASTF, g % HT_RING, full:full + P], psM[0:LASTF, full:full + P])
                            last.then_inc(s_ht, 1)

        @block.vector
        def _(dve):
            links = [0]

            def link(ins):
                links[0] += 1
                ins.then_inc(s_chain, 1)
                dve.wait_ge(s_chain, links[0])

            def mul(unit):
                t, j = divmod(unit, NU)
                b, lh = divmod(t, LH)
                if j == 0 and t >= 2:
                    dve.wait_ge(s_tr, NG * (t - 1))
                dve.wait_ge(s_ag, unit + 1)
                dst = hcat[:, t % 2, j * FF:(j + 1) * FF]
                up = psU[:, unit % 2, FF:2 * FF]
                if j < 2:
                    last = dve.tensor_tensor(dst, ag[:, unit % 2, :], up, ALU.mult)
                else:
                    if j == 2:
                        dve.wait_ge(s_w, b + 1)
                    last = dve.scalar_tensor_tensor(dst, up, wtok[:, b % 2, lh, j - 2:j - 1], ag[:, unit % 2, :],
                                                    ALU.mult, ALU.mult)
                last.then_inc(s_mul, 1)

            for task, i in order:
                if task == "load":
                    dve.memset(psA[:, :, :, 0:1], 0.0).then_inc(s_zero, 1)
                    dve.memset(minus_half[:, :], -0.5).then_inc(s_mh, 1)
                    dve.wait_ge(d_par, 16)
                    dve.tensor_scalar(cwh[:, :], par[:, PC_CONVW:PC_DTB], 0.5, None, ALU.mult).then_inc(s_half, 1)
                    dve.wait_ge(s_gt, 1)
                    dve.tensor_scalar(gates[:, :], gtanh[:, :], 0.5, None, ALU.mult).then_inc(s_gates, 1)
                    dve.wait_ge(s_aexp, 1)
                    dve.tensor_scalar(aneg[:, :], aexp[:, :], -1.0, None, ALU.mult).then_inc(s_aneg, 1)
                elif task == "conv":
                    dve.wait_ge(s_xh, EH * (i + 1))
                    if i == 0:
                        dve.wait_ge(s_half, 1)
                    for k in range(DC - 1):
                        back = DC - 1 - k
                        for h in range(EH):
                            done = EH * ((DC - 1) * i + k) + h
                            if k >= 1:
                                dve.wait_ge(s_tap, done - 1)
                            dve.scalar_tensor_tensor(xh[:, i % 2, h, back:L], psM[:, h * L:(h + 1) * L - back],
                                                     Wh[:, h, k:k + 1], xh[:, i % 2, h, back:L],
                                                     ALU.mult, ALU.add).then_inc(s_tap, 1)
                elif task == "silu_u":
                    dve.wait_ge(s_tu, i + 1)
                    if i >= 2:
                        dve.wait_ge(s_uD, EH * (i - 1))
                    dve.scalar_tensor_tensor(u[:, i % 2], tu[:, :, :], 1.0, xh[:, i % 2], ALU.add,
                                             ALU.mult).then_inc(s_u, 1)
                elif task == "split":
                    dve.wait_ge(s_hi, i + 1)
                    m1, m2 = 2 * 2 * DS, 2 * DS
                    dve.tensor_tensor(rest1[:, :], psM[0:m1, 0:L], parts[0:m1, i % 2, :], ALU.subtract).then_inc(s_rest, 1)
                    dve.wait_ge(s_rest, i + 1)
                    link(dve.tensor_copy(parts[0:m1, i % 2, :], rest1[:, :]))
                    link(dve.tensor_tensor(rest2[:, :], rest1[0:m2, :], parts[0:m2, i % 2, :], ALU.subtract))
                    dve.tensor_copy(parts[0:m2, i % 2, :], rest2[:, :]).then_inc(s_parts, 1)
                elif task == "delta":
                    dve.wait_ge(s_soft, 6 * i + 5)
                    link(dve.tensor_scalar(dy[:, :, :], dexp[:, :, :], 1.0, None, ALU.add))
                    link(dve.scalar_tensor_tensor(dnc[:, :, :], dy[:, :, :], -1.0, dexp[:, :, :], ALU.add, ALU.subtract))
                    link(dve.tensor_tensor(dsum[:, :, :], drel[:, :, :], dnc[:, :, :], ALU.subtract))
                    dve.wait_ge(s_soft, 6 * i + 6)
                    if i >= 2:
                        dve.wait_ge(s_dA, DS * (i - 1))
                        dve.wait_ge(s_dbu, DS * (i - 1))
                    dve.tensor_tensor(delta[:, i % 2], dln[:, :, :], dsum[:, :, :], ALU.add).then_inc(s_delta, 1)
                    dve.wait_ge(s_delta, i + 1)
                    dve.tensor_tensor(du[:, i % 2], delta[:, i % 2], u[:, i % 2], ALU.mult).then_inc(s_du, 1)
                elif task == "scan":
                    dve.wait_ge(s_dA, i + 1)
                    dve.wait_ge(s_dbu, i + 1)
                    if i >= 2:
                        dve.wait_ge(s_prod, i - 1)
                    flat = "p h l -> p (h l)"
                    dve.tensor_tensor_scan(hs[:, i % 2].rearrange(flat), psA[:, i % DA_RING].rearrange(flat),
                                           dbu[:, i % DBU_RING].rearrange(flat), 0.0, ALU.mult, ALU.add).then_inc(s_scan, 1)
                elif task == "prod":
                    dve.wait_ge(s_scan, i + 1)
                    dve.wait_ge(s_cps, i + 1)
                    if i >= PROD_RING:
                        j = i - PROD_RING
                        if j < DS:
                            dve.wait_ge(s_nsum, j + 1)
                        else:
                            dve.wait_ge(s_add, j - DS + 1)
                    dve.tensor_tensor(prod[:, i % PROD_RING], hs[:, i % 2], wide(psC[:, i % 2, 0:L], EH),
                                      ALU.mult).then_inc(s_prod, 1)
                elif task == "z_stats":
                    if i == 0:
                        dve.wait_ge(d_x0, 16)
                    if i == 1:
                        dve.wait_ge(d_x, 16 * (B - 1))
                    for h in range(LH):
                        dve.bn_stats(zst[:, i * LH + h, :], x_sb[:, i, h, :]).then_inc(s_zst, 1)
                    dve.wait_ge(s_zst, LH * (i + 1))
                    for h in range(LH):
                        dve.bn_aggr(zmv[:, i * LH + h, :], zst[:, i * LH + h, :]).then_inc(s_zmv, 1)
                elif task == "z_norm":
                    dve.wait_ge(s_zrs, i + 1)
                    dve.wait_ge(s_zmv, LH * (i + 1))
                    if i >= 1:
                        dve.wait_ge(s_zt, i)
                    for h in range(LH):
                        c = i * LH + h
                        dve.tensor_scalar(zn[:, h, :], x_sb[:, i, h, :], zmv[:, c, 0:1], zrs[:, c:c + 1],
                                          ALU.subtract, ALU.mult).then_inc(s_zn, 1)
                elif task == "z_gate":
                    dve.wait_ge(s_zt, i + 1)
                    dve.scalar_tensor_tensor(sz[:, i % 2], zt[:, :, :], 1.0, zn[:, :, :], ALU.add,
                                             ALU.mult).then_inc(s_sz, 1)
                elif task == "gate_y":
                    dve.wait_ge(s_sz, i + 1)
                    if i >= 1:
                        dve.wait_ge(s_yT, i)
                    if i == 0:
                        dve.wait_ge(s_nsum, DS)
                        dve.wait_ge(s_uD, EH)
                        dve.tensor_tensor(ysum[:, :, :], psD[:, :, :], uD[:, 0], ALU.add).then_inc(s_ys, 1)
                        dve.wait_ge(s_ys, 1)
                        y = ysum[:, :, :]
                    else:
                        dve.wait_ge(s_add, DS * i)
                        y = acc[:, i % 2]
                    dve.tensor_tensor(yg[:, :, :], y, sz[:, i % 2], ALU.mult).then_inc(s_yg, 1)
                elif task == "residual":
                    dve.wait_ge(s_yT, i + 1)
                    if i == 0:
                        dve.wait_ge(s_gates, 1)
                    dve.scalar_tensor_tensor(x2[:, i].rearrange("p h d -> p (h d)"), psM[:, :], gates[:, 0:1],
                                             x_sb[:, i].rearrange("p h d -> p (h d)"), ALU.mult, ALU.add).then_inc(s_x2, 1)
                    dve.wait_ge(s_x2, i + 1)
                    for h in range(LH):
                        dve.bn_stats(st2[:, h, :], x2[:, i, h, :]).then_inc(s_st2, 1)
                    dve.wait_ge(s_st2, LH * (i + 1))
                    if i >= 1:
                        dve.wait_ge(s_rs2, i)
                    for h in range(LH):
                        dve.bn_aggr(mv2[:, h, :], st2[:, h, :]).then_inc(s_mv2, 1)
                elif task == "norm":
                    dve.wait_ge(s_rs2, i + 1)
                    dve.wait_ge(s_mv2, LH * (i + 1))
                    if i >= 1:
                        dve.wait_ge(s_hT2, i)
                    for h in range(LH):
                        dve.tensor_scalar(hn[:, h, :], x2[:, i, h, :], mv2[:, h, 0:1], rs2[:, h:h + 1],
                                          ALU.subtract, ALU.mult).then_inc(s_hn, 1)
                elif task == "route":
                    dve.wait_ge(s_rex, i + 1)
                    link(dve.tensor_scalar(rs1[:, :], rex[:, :], 1.0, None, ALU.add))
                    link(dve.reciprocal(score[:, :], rs1[:, :]))
                    for h in range(LH):
                        last = dve.max(top[:, h, :], score[:, h * NE:(h + 1) * NE])
                    link(last)
                    for h in range(LH):
                        last = dve.max_index(topi[:, h, :], top[:, h, :], score[:, h * NE:(h + 1) * NE])
                    link(last)
                    dve.tensor_copy(topf[:, :, :], topi[:, :, 0:2])
                    link(dve.scalar_tensor_tensor(den[:, :], top[:, :, 0], 1e-20, top[:, :, 1], ALU.add, ALU.add))
                    link(dve.reciprocal(rden[:, :], den[:, :]))
                    link(dve.scalar_tensor_tensor(topw[:, :, :], top[:, :, 0:2], SCALE,
                                                  rden[:, :].unsqueeze(2).broadcast_to([P, LH, 2]), ALU.mult, ALU.mult))
                    for h in range(LH):
                        for r in range(2):
                            last = dve.tensor_scalar(pick[:, h, r, :], par[:, PC_IOTA:PC_IOTA + NE], topf[:, h, r:r + 1],
                                                     topw[:, h, r:r + 1], ALU.is_equal, ALU.mult)
                    link(last)
                    dve.tensor_tensor(wtok[:, i % 2], pick[:, :, 0, :], pick[:, :, 1, :], ALU.add).then_inc(s_w, 1)
                elif task == "mul":
                    mul(i)
                if task in ("gate", "flush"):
                    for unit in ([i] if task == "gate" else range(UNITS, UNITS + 4)):
                        if unit < UNITS:
                            dve.wait_ge(s_tanh, unit + 1)
                            dve.scalar_tensor_tensor(ag[:, unit % 2, :], tg[:, unit % 2, :], 1.0,
                                                     psU[:, unit % 2, 0:FF], ALU.add, ALU.mult).then_inc(s_ag, 1)
                        for g in groups_after(unit, 4):
                            t, q = divmod(g, NG)
                            if q == NG - 1:
                                b, lh = divmod(t, LH)
                                dve.wait_ge(s_dn, g + 1)
                                if t >= 2:
                                    dve.wait_ge(d_out[t % 2], 16 * (t // 2))
                                dve.scalar_tensor_tensor(outb[:, t % 2, :], psD[:, 0, :], gates[:, 1:2],
                                                         x2[:, b, lh, :], ALU.mult, ALU.add).then_inc(s_fin, 1)

        @block.gpsimd
        def _(pool):
            def times_b(m):
                b, n = divmod(m, DS)
                if n == 0:
                    pool.wait_ge(s_du, b + 1)
                if m % 2 == 0:
                    pool.wait_ge(s_bb, m // 2 + 1)
                if m >= DBU_RING:
                    pool.wait_ge(s_scan, m - DBU_RING + 1)
                pool.tensor_tensor(dbu[:, m % DBU_RING], du[:, b % 2], wide(bb[:, m // 2 % BB_RING, m % 2, :], EH),
                                   ALU.mult).then_inc(s_dbu, 1)

            for task, i in order:
                if task == "first":
                    times_b(0)
                elif task == "scan":
                    if i + 1 < B * DS:
                        times_b(i + 1)
                elif task == "prod" and i >= DS:
                    b, n = divmod(i, DS)
                    pool.wait_ge(s_prod, i + 1)
                    if n == 0:
                        pool.wait_ge(s_uD, EH * (b + 1))
                        if b >= 2:
                            pool.wait_ge(s_yg, b - 1)
                        before = uD[:, b % 2]
                    else:
                        pool.wait_ge(s_add, i - DS)
                        before = acc[:, b % 2]
                    pool.tensor_tensor(acc[:, b % 2], before, prod[:, i % PROD_RING], ALU.add).then_inc(s_add, 1)
                elif task == "z_stats":
                    pool.wait_ge(s_zmv, LH * (i + 1))
                    if i == 0:
                        pool.wait_ge(s_mh, 1)
                    c = slice(i * LH, (i + 1) * LH)
                    pool.tensor_scalar(zve[:, c], zmv[:, c, 1], EPS, None, ALU.add).then_inc(s_zve, 1)
                    pool.wait_ge(s_zve, i + 1)
                    pool.tensor_tensor(zrs[:, c], zve[:, c], minus_half[:, c], ALU.pow).then_inc(s_zrs, 1)
                elif task == "residual":
                    pool.wait_ge(s_mv2, LH * (i + 1))
                    if i >= 1:
                        pool.wait_ge(s_hn, LH * i)
                    pool.tensor_scalar(ve2[:, :], mv2[:, :, 1], EPS, None, ALU.add).then_inc(s_ve2, 1)
                    pool.wait_ge(s_ve2, i + 1)
                    pool.tensor_tensor(rs2[:, :], ve2[:, :], minus_half[:, 0:LH], ALU.pow).then_inc(s_rs2, 1)


def kernel(**inputs):
    import concourse.bacc as bacc
    import ml_dtypes
    from concourse.bass_utils import run_bass_kernel_spmd

    a = {k: np.asarray(v) for k, v in inputs.items()}

    def halves(w):
        return w.reshape(w.shape[0], -1, P).transpose(2, 1, 0)

    def channels(w):
        return w.reshape(EH, P, -1).transpose(1, 0, 2).reshape(P, -1)

    params = np.concatenate([
        channels(a["L0_xattn_conv_w"]), channels(a["L0_xattn_conv_b"]), channels(a["L0_xattn_dt_proj_b"]),
        channels(a["L0_xattn_D"]), channels(a["L0_xattn_A_log"]),
        np.broadcast_to(a["g_xattn"].reshape(1, 1), (P, 1)), np.broadcast_to(a["g_ffn"].reshape(1, 1), (P, 1)),
        np.broadcast_to(np.arange(NE, dtype=np.float32), (P, NE))], axis=1)
    wx = a["L0_xattn_x_proj_w"]
    gate = np.concatenate([a["L0_ffn_shared_wg"].reshape(2, FF, D), a["L0_ffn_exp_wg"]])
    up = np.concatenate([a["L0_ffn_shared_wu"].reshape(2, FF, D), a["L0_ffn_exp_wu"]])
    both = np.concatenate([gate, up], axis=1)
    rows = np.arange(XROWS) % (2 * DS)
    arrays = {
        "ctxT": a["ctx_1024"].transpose(2, 0, 1),
        "x": a["x"],
        "params": params,
        "w_in": a["L0_xattn_in_proj_w"].T,
        "w_x": halves(np.concatenate([wx[DR:], wx[DR:], wx[DR:], wx[:DR]])),
        "w_dt": a["L0_xattn_dt_proj_w"].T,
        "w_gate": halves(a["L0_ffn_gate_w"]),
        "w_up": both.reshape(NU, 2 * FF, KT, P).transpose(3, 2, 0, 1),
        "w_down": np.concatenate([a["L0_ffn_shared_wd"].T, a["L0_ffn_exp_wd"].transpose(0, 2, 1).reshape(NE * FF, D)]),
        "ident": np.eye(P, dtype=np.float32),
        "sel": np.broadcast_to((rows[:, None] == np.arange(2 * DS))[:, :, None], (XROWS, 2 * DS, P)).astype(ml_dtypes.bfloat16),
    }
    arrays = {f"in_{k}": np.ascontiguousarray(v) for k, v in arrays.items()}
    nc = bacc.Bacc("TRN2", target_bir_lowering=False, num_devices=1)
    args = [nc.dram_tensor(k, v.shape, mybir.dt.from_np(v.dtype), kind="ExternalInput").ap() for k, v in arrays.items()]
    out = nc.dram_tensor("out_0", (B, L, D), F32, kind="ExternalOutput").ap()
    mixer(nc, *args, out)
    return run_bass_kernel_spmd(nc, [arrays], core_ids=[0]).results[0]["out_0"]
```

```python
from contextlib import ExitStack

import numpy as np

import concourse.bass as bass
from concourse import mybir

F32 = mybir.dt.float32
BF16 = mybir.dt.bfloat16
U32 = mybir.dt.uint32
ALU = mybir.AluOpType
ACT = mybir.ActivationFunctionType

P = 128
B, L, D = 4, 256, 256
DM, DI, DS, DC, DR = 128, 256, 16, 4, 8
EH = DI // P
LH = L // P
KT = D // P
NE, FF = 8, 176
NU = NE + 2
FCAT = NU * FF
FB = (FCAT + P - 1) // P
LASTF = FCAT - (FB - 1) * P
SCALE = 2.5
EPS = 1e-5

PC_CONVW = 0
PC_CONVB = PC_CONVW + EH * DC
PC_DTB = PC_CONVB + EH
PC_D = PC_DTB + EH
PC_ALOG = PC_D + EH
PC_GX = PC_ALOG + EH * DS
PC_GF = PC_GX + 1
PC_IOTA = PC_GF + 1
NPC = PC_IOTA + NE

XROWS = 3 * 2 * DS
XM = XROWS + DR

DA_RING, DBU_RING, PROD_RING, HT_RING = 2, 3, 3, 3

UNITS = B * LH * NU
FIRST_UNIT = 6
GROUPS = [(0, 4), (4, 8), (8, 12), (12, FB)]
NG = len(GROUPS)


def group_last_unit(g):
    return (min(GROUPS[g][1] * P, FCAT) - 1) // FF


def schedule():
    steps = B * DS
    before = {3: (["project"], ["project_out"], []), 4: ([], [], ["tap0"]), 5: ([], [], ["tap1"]),
              6: ([], [], ["tap2"]), 7: ([], ["tanh_u"], ["silu_u"]), 8: (["xproj"], ["xproj_out"], []),
              9: (["dt"], ["dt_out"], ["split"]), 10: ([], ["softplus"], []), 11: ([], ["skip"], ["delta"])}
    behind = {2: (["to_tokens"], [], ["residual"]), 3: ([], [], ["norm"]),
              4: (["to_features"], ["to_features_out"], []), 5: (["logits"], ["logits_out"], []), 6: ([], [], ["route"])}
    z = {0: ["z_stats"], 12: ["z_norm"], 14: ["z_gate"]}
    order = [("load", 0)]
    for n in sorted(before):
        order += [(t, 0) for part in before[n] for t in part]
    order += [("first", 0), ("spread_b", 0)]
    unit_at = {}
    for u in range(UNITS):
        b, j = divmod(u, LH * NU)
        unit_at.setdefault(DS * (b + 1) + FIRST_UNIT + j * DS // (LH * NU), []).append(u)
    for s in range(DS * (B + 1) + FIRST_UNIT + DS):
        b, n = divmod(s, DS)
        units = unit_at.get(s, [])
        if units:
            order.append(("up", units[0]))
        if 1 <= s <= steps:
            order.append(("spread_c", s - 1))
        if units:
            order.append(("gate", units[0]))
        fill, read, follow = [], [], []
        for table, of in ((behind, b - 1), (before, b + 1)):
            if 0 <= of < B and n in table:
                for a, part in zip((fill, read, follow), table[n]):
                    a += [(t, of) for t in part]
        if 1 <= b <= B and n == 1:
            follow.append(("gate_y", b - 1))
        if b < B and n in z:
            follow += [(t, b) for t in z[n]]
        order += fill
        if s < steps:
            order.append(("scan", s))
        if units:
            order.append(("mul", units[0]))
        order += read
        if 1 <= s <= steps:
            order.append(("prod", s - 1))
        order += follow
        if s % 2 == 0 and s + 2 < DS:
            order.append(("spread_b", s // 2 + 1))
        for u in units[1:]:
            order += [("up", u), ("gate", u), ("mul", u)]
    return order + [("flush", UNITS)]


def mixer(nc, ctxT, x, params, w_in, w_x, w_dt, w_gate, w_up, w_down, ident_in, sel_in, out):
    order = schedule()
    with ExitStack() as stack:
        def sb(name, shape, dt=F32):
            return stack.enter_context(nc.sbuf_tensor(name, shape, dt))

        def ps(name, shape, dt=F32):
            return stack.enter_context(nc.psum_tensor(name, shape, dt))

        def sem(name):
            return stack.enter_context(nc.semaphore(name))

        ctx_sb = sb("ctx_sb", [P, B, L])
        x_sb = sb("x_sb", [P, B, LH, D])
        par = sb("par", [P, NPC])
        win = sb("win", [P, DI])
        wx = sb("wx", [P, EH, XM])
        wdt = sb("wdt", [P, DI])
        wg = sb("wg", [P, KT, NE])
        wup = sb("wup", [P, KT, NU, 2 * FF])
        wdn = sb("wdn", [P, FB, D])
        ident = sb("ident", [P, P])
        sel = sb("sel", [P, 2 * DS, P], BF16)
        cwh = sb("cwh", [P, EH * DC + EH])
        aneg = sb("aneg", [P, EH * DS])
        aexp = sb("aexp", [P, EH * DS])
        gtanh = sb("gtanh", [P, 2])
        gates = sb("gates", [P, 2])
        minus_half = sb("minus_half", [P, B * LH])
        zst = sb("zst", [P, B * LH, 6])
        zmv = sb("zmv", [P, B * LH, 2])
        zve = sb("zve", [P, B * LH])
        zrs = sb("zrs", [P, B * LH])
        zn = sb("zn", [P, LH, L])
        zt = sb("zt", [P, LH, L])
        sz = sb("sz", [P, 2, LH, L])
        xh = sb("xh", [P, 2, EH, L])
        tu = sb("tu", [P, EH, L])
        u = sb("u", [P, 2, EH, L])
        xraw = sb("xraw", [P, EH, L])
        xdbl = sb("xdbl", [P, L])
        parts = sb("parts", [XROWS, 2, L], BF16)
        rest1 = sb("rest1", [2 * 2 * DS, L])
        rest2 = sb("rest2", [2 * DS, L])
        dabs = sb("dabs", [P, EH, L])
        dexp = sb("dexp", [P, EH, L])
        dln = sb("dln", [P, EH, L])
        drel = sb("drel", [P, EH, L])
        dy = sb("dy", [P, EH, L])
        dnc = sb("dnc", [P, EH, L])
        dsum = sb("dsum", [P, EH, L])
        delta = sb("delta", [P, 2, EH, L])
        du = sb("du", [P, 2, EH, L])
        uD = sb("uD", [P, 2, EH, L])
        bb = sb("bb", [P, 2, DS, L])
        dbu = sb("dbu", [P, DBU_RING, EH, L])
        hs = sb("hs", [P, 2, EH, L])
        prod = sb("prod", [P, PROD_RING, EH, L])
        acc = sb("acc", [P, 2, EH, L])
        ysum = sb("ysum", [P, EH, L])
        yg = sb("yg", [P, EH, L])
        x2 = x_sb
        st2 = sb("st2", [P, LH, 6])
        mv2 = sb("mv2", [P, LH, 2])
        ve2 = sb("ve2", [P, LH])
        rs2 = sb("rs2", [P, LH])
        hn = sb("hn", [P, LH, D])
        hnT = sb("hnT", [P, 2, KT, L])
        rex = sb("rex", [P, LH * NE])
        rs1 = sb("rs1", [P, LH * NE])
        score = sb("score", [P, LH * NE])
        top = sb("top", [P, LH, 8])
        topi = sb("topi", [P, LH, 8], U32)
        topf = sb("topf", [P, LH, 2])
        den = sb("den", [P, LH])
        rden = sb("rden", [P, LH])
        topw = sb("topw", [P, LH, 2])
        pick = sb("pick", [P, LH, 2, NE])
        wtok = sb("wtok", [P, 2, LH, NE])
        tg = sb("tg", [P, 2, FF])
        ag = sb("ag", [P, 2, FF])
        hcat = sb("hcat", [P, 2, FCAT])
        hT = sb("hT", [P, HT_RING, 4 * P])
        outb = sb("outb", [P, 2, D])

        brows = nc.dram_tensor("brows", (B, DS, L), F32).ap()

        psA = ps("psA", [P, DA_RING, EH, L])
        psC = ps("psC", [P, 2, 512])
        psM = ps("psM", [P, 512])
        psU = ps("psU", [P, 2, 512])
        psD = ps("psD", [P, 2, D])

        d_par, d_ctx0, d_ctx, d_win, d_wx = sem("d_par"), sem("d_ctx0"), sem("d_ctx"), sem("d_win"), sem("d_wx")
        d_wdt, d_id, d_sel, d_x0, d_x = sem("d_wdt"), sem("d_id"), sem("d_sel"), sem("d_x0"), sem("d_x")
        d_wg, d_wup, d_wdn = sem("d_wg"), sem("d_wup"), sem("d_wdn")
        d_brow, d_bb = sem("d_brow"), sem("d_bb")
        d_out = [sem("d_out0"), sem("d_out1")]
        s_half, s_aexp, s_aneg, s_gt, s_gates = sem("s_half"), sem("s_aexp"), sem("s_aneg"), sem("s_gt"), sem("s_gates")
        s_mh, s_zero = sem("s_mh"), sem("s_zero")
        s_zst, s_zmv, s_zve, s_zrs, s_zn, s_zt, s_sz = (sem("s_zst"), sem("s_zmv"), sem("s_zve"), sem("s_zrs"),
                                                       sem("s_zn"), sem("s_zt"), sem("s_sz"))
        s_xin, s_xh, s_tap, s_tu, s_u = sem("s_xin"), sem("s_xh"), sem("s_tap"), sem("s_tu"), sem("s_u")
        s_xdbl, s_xd, s_hi, s_rest, s_parts = sem("s_xdbl"), sem("s_xd"), sem("s_hi"), sem("s_rest"), sem("s_parts")
        s_dtp, s_soft, s_del, s_delta, s_du, s_uD = (sem("s_dtp"), sem("s_soft"), sem("s_del"), sem("s_delta"),
                                                    sem("s_du"), sem("s_uD"))
        s_bps, s_bb, s_cps, s_dA, s_dbu = sem("s_bps"), sem("s_bb"), sem("s_cps"), sem("s_dA"), sem("s_dbu")
        s_scan, s_prod, s_add, s_nsum = sem("s_scan"), sem("s_prod"), sem("s_add"), sem("s_nsum")
        s_ys, s_yg, s_yT, s_x2, s_st2, s_mv2, s_ve2, s_rs2 = (sem("s_ys"), sem("s_yg"), sem("s_yT"), sem("s_x2"),
                                                             sem("s_st2"), sem("s_mv2"), sem("s_ve2"), sem("s_rs2"))
        s_hn, s_hT2, s_hnT, s_log, s_rex, s_rt, s_w = (sem("s_hn"), sem("s_hT2"), sem("s_hnT"), sem("s_log"),
                                                       sem("s_rex"), sem("s_rt"), sem("s_w"))
        s_up, s_tanh, s_ag, s_mul, s_tr, s_ht, s_dn, s_fin = (sem("s_up"), sem("s_tanh"), sem("s_ag"), sem("s_mul"),
                                                             sem("s_tr"), sem("s_ht"), sem("s_dn"), sem("s_fin"))
        s_chain = sem("s_chain")

        Wh = cwh[:, 0:EH * DC].rearrange("p (h k) -> p h k", h=EH)

        def wide(ap, n):
            return ap.unsqueeze(1).broadcast_to([ap.shape[0], n, ap.shape[1]])

        def on_pe(m):
            return m < DS - 2 and m % 2 == 1

        def added(m):
            if on_pe(m):
                return s_nsum, m // 2 + 1
            return s_add, m + 1 - sum(on_pe(j) for j in range(m))

        def groups_after(unit, lag):
            u0 = unit - lag
            if u0 < 0 or u0 >= UNITS:
                return []
            t, j = divmod(u0, NU)
            return [NG * t + g for g in range(NG) if group_last_unit(g) == j]

        block = stack.enter_context(nc.Block())

        @block.sync
        def _(sp):
            sp.dma_start(ctx_sb[:, 0, :], ctxT[:, 0, :]).then_inc(d_ctx0, 16)
            sp.dma_start(wx[:, :, :], w_x).then_inc(d_wx, 16)
            sp.dma_start(sel[0:XROWS, :, :], sel_in).then_inc(d_sel, 16)
            sp.dma_start(x_sb[:, 0], x[0].rearrange("(h p) d -> p h d", p=P)).then_inc(d_x0, 16)
            sp.dma_start(ctx_sb[:, 1:B, :], ctxT[:, 1:B, :]).then_inc(d_ctx, 16)
            for b in range(1, B):
                sp.dma_start(x_sb[:, b], x[b].rearrange("(h p) d -> p h d", p=P)).then_inc(d_x, 16)
            sp.dma_start(wg[:, :, :], w_gate).then_inc(d_wg, 16)
            for k in range(KT):
                sp.dma_start(wup[:, k], w_up[:, k]).then_inc(d_wup, 16)
            sp.dma_start(wdn[:, 0:FB - 1, :], w_down[0:(FB - 1) * P].rearrange("(f p) d -> p f d", p=P)).then_inc(d_wdn, 16)
            sp.dma_start(wdn[0:LASTF, FB - 1, :], w_down[(FB - 1) * P:FCAT]).then_inc(d_wdn, 16)
            for task, i in order:
                if task == "xproj" and i >= 1:
                    sp.wait_ge(s_xd, i + 1)
                    sp.dma_start(brows[i], xdbl[0:DS, :]).then_inc(d_brow, 16)
                elif task == "dt" and i >= 1:
                    sp.wait_ge(d_brow, 16 * i)
                    if i >= 2:
                        sp.wait_ge(s_dbu, DS * (i - 1))
                    sp.dma_start(bb[:, i % 2], brows[i].unsqueeze(0).broadcast_to([P, DS, L])).then_inc(d_bb, 16)
                elif task in ("gate", "flush"):
                    for unit in ([i] if task == "gate" else range(UNITS, UNITS + 4)):
                        for g in groups_after(unit, 4):
                            t, q = divmod(g, NG)
                            if q == NG - 1:
                                b, h = divmod(t, LH)
                                sp.wait_ge(s_fin, t + 1)
                                sp.dma_start(out[b, h * P:(h + 1) * P, :], outb[:, t % 2, :]).then_inc(d_out[t % 2], 16)
            for q in d_out:
                sp.wait_ge(q, 16 * B * LH // 2)

        @block.tensor
        def _(pe):
            psM_read = []

            def take_misc(reader, value):
                if psM_read:
                    pe.wait_ge(*psM_read.pop())
                psM_read.append((reader, value))

            def spread_b(k):
                b = 2 * k // DS
                take_misc(s_bb, k + 1)
                pe.wait_ge(s_parts, b + 1)
                for i in range(2):
                    last = pe.matmul(psM[:, i * L:(i + 1) * L], sel[0:XROWS, (2 * k + i) % DS, :], parts[:, b % 2, :],
                                     start=True, stop=True)
                last.then_inc(s_bps, 1)

            for task, i in order:
                if task == "project":
                    take_misc(s_xh, (EH + 1) * (i + 1))
                    if i == 0:
                        pe.wait_ge(d_ctx0, 16)
                        pe.wait_ge(d_win, 16)
                    if i == 1:
                        pe.wait_ge(d_ctx, 16)
                    for h in range(EH):
                        last = pe.matmul(psM[:, h * L:(h + 1) * L], win[:, h * P:(h + 1) * P], ctx_sb[:, i, :],
                                         start=True, stop=True)
                    last.then_inc(s_xin, 1)
                elif task == "xproj":
                    take_misc(s_xd, i + 1)
                    if i == 0:
                        pe.wait_ge(d_wx, 16)
                    pe.wait_ge(s_u, i + 1)
                    for h in range(EH):
                        last = pe.matmul(psM[0:XM, 0:L], wx[:, h, :], u[:, i % 2, h, :], start=(h == 0), stop=(h == EH - 1))
                    last.then_inc(s_xdbl, 1)
                elif task == "dt":
                    take_misc(s_soft, 6 * i + 4)
                    if i == 0:
                        pe.wait_ge(d_wdt, 16)
                    pe.wait_ge(s_xd, i + 1)
                    for h in range(EH):
                        last = pe.matmul(psM[:, h * L:(h + 1) * L], wdt[XROWS:XM, h * P:(h + 1) * P],
                                         xdbl[XROWS:XM, :], start=True, stop=True)
                    last.then_inc(s_dtp, 1)
                elif task == "spread_b":
                    if i == 0:
                        pe.wait_ge(d_sel, 16)
                    spread_b(i)
                elif task == "spread_c":
                    b, n = divmod(i, DS)
                    if i == 0:
                        pe.wait_ge(d_sel, 16)
                    if i % DS == 0:
                        pe.wait_ge(s_parts, b + 1)
                    if i >= 2:
                        pe.wait_ge(s_prod, i - 1)
                    pe.matmul(psC[:, i % 2, 0:L], sel[0:XROWS, DS + n, :], parts[:, b % 2, :],
                              start=True, stop=True).then_inc(s_cps, 1)
                    if i >= 2 and on_pe(i - 2):
                        if i - 2 == 1:
                            pe.wait_ge(d_id, 16)
                        pe.wait_ge(s_prod, i - 1)
                        pe.matmul(psD[:, :, :], ident[:, :], prod[:, (i - 2) % PROD_RING], start=(i - 2 == 1),
                                  stop=(i - 2 == DS - 3)).then_inc(s_nsum, 1)
                elif task == "to_tokens":
                    take_misc(s_x2, i + 1)
                    pe.wait_ge(s_yg, i + 1)
                    for lh in range(LH):
                        for h in range(EH):
                            last = pe.transpose(psM[:, lh * D + h * P:lh * D + (h + 1) * P],
                                                yg[:, h, lh * P:(lh + 1) * P], ident[:, :])
                    last.then_inc(s_yT, 1)
                elif task == "to_features":
                    take_misc(s_hnT, i + 1)
                    pe.wait_ge(s_hn, LH * (i + 1))
                    for k in range(KT):
                        for lh in range(LH):
                            last = pe.transpose(psM[:, k * L + lh * P:k * L + (lh + 1) * P],
                                                hn[:, lh, k * P:(k + 1) * P], ident[:, :])
                    last.then_inc(s_hT2, 1)
                elif task == "logits":
                    take_misc(s_rex, i + 1)
                    if i == 0:
                        pe.wait_ge(d_wg, 16)
                    pe.wait_ge(s_hnT, i + 1)
                    for lh in range(LH):
                        for k in range(KT):
                            last = pe.matmul(psM[:, lh * NE:(lh + 1) * NE], hnT[:, i % 2, k, lh * P:(lh + 1) * P],
                                             wg[:, k, :], start=(k == 0), stop=(k == KT - 1))
                    last.then_inc(s_log, 1)
                if task in ("up", "flush"):
                    for unit in ([i] if task == "up" else range(UNITS, UNITS + 4)):
                        if unit < UNITS:
                            t, j = divmod(unit, NU)
                            b, lh = divmod(t, LH)
                            if unit == 0:
                                pe.wait_ge(d_wup, 16 * KT)
                            pe.wait_ge(s_hnT, b + 1)
                            if unit >= 2:
                                pe.wait_ge(s_mul, unit - 1)
                            for k in range(KT):
                                last = pe.matmul(psU[:, unit % 2, 0:2 * FF], hnT[:, b % 2, k, lh * P:(lh + 1) * P],
                                                 wup[:, k, j, :], start=(k == 0), stop=(k == KT - 1))
                            last.then_inc(s_up, 1)
                        for g in groups_after(unit, 2):
                            t, q = divmod(g, NG)
                            take_misc(s_ht, g + 1)
                            pe.wait_ge(s_mul, unit - 1)
                            for f in range(*GROUPS[q]):
                                m = P if f < FB - 1 else LASTF
                                c = (f - GROUPS[q][0]) * P
                                last = pe.transpose(psM[0:m, c:c + P], hcat[:, t % 2, f * P:f * P + m], ident[:, :])
                            last.then_inc(s_tr, 1)
                        for g in groups_after(unit, 3):
                            t, q = divmod(g, NG)
                            if g == 0:
                                pe.wait_ge(d_wdn, 32)
                            if q == 0 and t >= 1:
                                pe.wait_ge(s_fin, t)
                            if q == 0 and t == 0:
                                pe.wait_ge(s_ys, 1)
                            pe.wait_ge(s_ht, g + 1)
                            for f in range(*GROUPS[q]):
                                m = P if f < FB - 1 else LASTF
                                c = (f - GROUPS[q][0]) * P
                                last = pe.matmul(psD[:, 0, :], hT[0:m, g % HT_RING, c:c + P], wdn[0:m, f, :],
                                                 start=(f == 0), stop=(f == FB - 1))
                            last.then_inc(s_dn, 1)

        @block.scalar
        def _(act):
            act.dma_start(par[:, :], params).then_inc(d_par, 16)
            act.dma_start(win[:, :], w_in).then_inc(d_win, 16)
            act.dma_start(wdt[XROWS:XM, :], w_dt).then_inc(d_wdt, 16)
            act.dma_start(ident[:, :], ident_in).then_inc(d_id, 16)

            def exps(m):
                b, n = divmod(m, DS)
                if n == 0:
                    act.wait_ge(s_delta, b + 1)
                if m == 0:
                    act.wait_ge(s_aneg, 1)
                    act.wait_ge(s_zero, 1)
                if m >= DA_RING:
                    act.wait_ge(s_scan, m - DA_RING + 1)
                for h in range(EH):
                    last = act.activation(psA[:, m % DA_RING, h, 1:L], delta[:, b % 2, h, 1:L], ACT.Exp,
                                          scale=aneg[:, h * DS + n:h * DS + n + 1])
                last.then_inc(s_dA, 1)

            def copy_b(k):
                act.wait_ge(s_bps, k + 1)
                act.copy(bb[:, 0, 2 * k:2 * k + 2, :].rearrange("p s l -> p (s l)"), psM[:, :]).then_inc(s_bb, 1)

            for task, i in order:
                if task == "load":
                    act.wait_ge(d_par, 16)
                    act.activation(gtanh[:, :], par[:, PC_GX:PC_GX + 2], ACT.Tanh).then_inc(s_gt, 1)
                    act.activation(aexp[:, :], par[:, PC_ALOG:PC_ALOG + EH * DS], ACT.Exp).then_inc(s_aexp, 1)
                elif task == "project_out":
                    act.wait_ge(s_xin, i + 1)
                    if i == 0:
                        act.wait_ge(s_half, 1)
                    if i >= 2:
                        act.wait_ge(s_u, i - 1)
                    for h in range(EH):
                        act.activation(xh[:, i % 2, h, :], psM[:, h * L:(h + 1) * L], ACT.Identity,
                                       scale=Wh[:, h, DC - 1:DC],
                                       bias=cwh[:, EH * DC + h:EH * DC + h + 1]).then_inc(s_xh, 1)
                    if i >= 1:
                        act.wait_ge(s_tap, EH * (DC - 1) * i)
                    act.copy(xraw[:, :, :].rearrange("p h l -> p (h l)"), psM[:, :]).then_inc(s_xh, 1)
                elif task == "tanh_u":
                    act.wait_ge(s_tap, EH * (DC - 1) * (i + 1))
                    if i >= 1:
                        act.wait_ge(s_u, i)
                    act.activation(tu[:, :, :], xh[:, i % 2], ACT.Tanh).then_inc(s_tu, 1)
                elif task == "xproj_out":
                    act.wait_ge(s_xdbl, i + 1)
                    if i >= 1:
                        act.wait_ge(s_dtp, i)
                        act.wait_ge(s_rest, i)
                    if i >= 2:
                        act.wait_ge(d_brow, 16 * (i - 1))
                    act.copy(xdbl[0:XM, :], psM[0:XM, 0:L]).then_inc(s_xd, 1)
                    if i >= 2:
                        act.wait_ge(s_cps, DS * (i - 1))
                    if i == 2:
                        act.wait_ge(s_bps, DS // 2)
                    act.wait_ge(s_xd, i + 1)
                    act.copy(parts[:, i % 2, :], xdbl[0:XROWS, :]).then_inc(s_hi, 1)
                elif task == "dt_out":
                    act.wait_ge(s_dtp, i + 1)
                    if i >= 1:
                        act.wait_ge(s_delta, i)
                    for h in range(EH):
                        act.activation(dabs[:, h, :], psM[:, h * L:(h + 1) * L], ACT.Abs,
                                       bias=par[:, PC_DTB + h:PC_DTB + h + 1]).then_inc(s_soft, 1)
                    for h in range(EH):
                        last = act.activation(drel[:, h, :], psM[:, h * L:(h + 1) * L], ACT.Relu,
                                              bias=par[:, PC_DTB + h:PC_DTB + h + 1])
                        last.then_inc(s_soft, 1)
                elif task == "softplus":
                    act.preload_act_table_set("natural_log_exp_and_others")
                    act.wait_ge(s_soft, 6 * i + 2)
                    act.activation(dexp[:, :, :], dabs[:, :, :], ACT.Exp, scale=-1.0).then_inc(s_soft, 1)
                    act.wait_ge(s_soft, 6 * i + 5)
                    act.activation(dln[:, :, :], dexp[:, :, :], ACT.Ln, bias=1.0).then_inc(s_soft, 1)
                elif task == "skip":
                    if i >= 2:
                        act.wait_ge(*added(DS * (i - 2)))
                    for h in range(EH):
                        act.activation(uD[:, i % 2, h, :], u[:, i % 2, h, :], ACT.Copy,
                                       scale=par[:, PC_D + h:PC_D + h + 1]).then_inc(s_uD, 1)
                elif task == "spread_b":
                    copy_b(i)
                elif task == "first":
                    exps(0)
                elif task == "scan":
                    if i + 1 < B * DS:
                        exps(i + 1)
                elif task == "z_gate":
                    act.wait_ge(s_zn, LH * (i + 1))
                    if i >= 1:
                        act.wait_ge(s_sz, i)
                    act.activation(zt[:, :, :], zn[:, :, :], ACT.Tanh, scale=0.5).then_inc(s_zt, 1)
                elif task == "to_features_out":
                    act.wait_ge(s_hT2, i + 1)
                    if i >= 2:
                        act.wait_ge(s_up, LH * NU * (i - 1))
                    act.copy(hnT[:, i % 2, :, :].rearrange("p k l -> p (k l)"), psM[:, :]).then_inc(s_hnT, 1)
                elif task == "logits_out":
                    act.wait_ge(s_log, i + 1)
                    if i >= 1:
                        act.wait_ge(s_w, i)
                    act.activation(rex[:, :], psM[:, 0:LH * NE], ACT.Exp, scale=-1.0).then_inc(s_rex, 1)
                if task in ("up", "flush"):
                    for unit in ([i] if task == "up" else range(UNITS, UNITS + 4)):
                        if unit < UNITS:
                            act.wait_ge(s_up, unit + 1)
                            if unit >= 2:
                                act.wait_ge(s_ag, unit - 1)
                            act.activation(tg[:, unit % 2, :], psU[:, unit % 2, 0:FF], ACT.Tanh,
                                           scale=0.5).then_inc(s_tanh, 1)
                        for g in groups_after(unit, 2):
                            q = g % NG
                            act.wait_ge(s_tr, g + 1)
                            if g >= HT_RING:
                                act.wait_ge(s_dn, g - HT_RING + 1)
                            full = sum(1 for f in range(*GROUPS[q]) if f < FB - 1) * P
                            last = act.copy(hT[:, g % HT_RING, 0:full], psM[:, 0:full])
                            if q == NG - 1:
                                last = act.copy(hT[0:LASTF, g % HT_RING, full:full + P], psM[0:LASTF, full:full + P])
                            last.then_inc(s_ht, 1)

        @block.vector
        def _(dve):
            links = [0]

            def link(ins):
                links[0] += 1
                ins.then_inc(s_chain, 1)
                dve.wait_ge(s_chain, links[0])

            def mul(unit):
                t, j = divmod(unit, NU)
                b, lh = divmod(t, LH)
                if j == 0 and t >= 2:
                    dve.wait_ge(s_tr, NG * (t - 1))
                dve.wait_ge(s_ag, unit + 1)
                dst = hcat[:, t % 2, j * FF:(j + 1) * FF]
                up = psU[:, unit % 2, FF:2 * FF]
                if j < 2:
                    last = dve.tensor_tensor(dst, ag[:, unit % 2, :], up, ALU.mult)
                else:
                    if j == 2:
                        dve.wait_ge(s_w, b + 1)
                    last = dve.scalar_tensor_tensor(dst, up, wtok[:, b % 2, lh, j - 2:j - 1], ag[:, unit % 2, :],
                                                    ALU.mult, ALU.mult)
                last.then_inc(s_mul, 1)

            for task, i in order:
                if task == "load":
                    dve.memset(psA[:, :, :, 0:1], 0.0).then_inc(s_zero, 1)
                    dve.memset(minus_half[:, :], -0.5).then_inc(s_mh, 1)
                    dve.wait_ge(d_par, 16)
                    dve.tensor_scalar(cwh[:, :], par[:, PC_CONVW:PC_DTB], 0.5, None, ALU.mult).then_inc(s_half, 1)
                    dve.wait_ge(s_gt, 1)
                    dve.tensor_scalar(gates[:, :], gtanh[:, :], 0.5, None, ALU.mult).then_inc(s_gates, 1)
                    dve.wait_ge(s_aexp, 1)
                    dve.tensor_scalar(aneg[:, :], aexp[:, :], -1.0, None, ALU.mult).then_inc(s_aneg, 1)
                elif task in ("tap0", "tap1", "tap2"):
                    k = int(task[-1])
                    back = DC - 1 - k
                    dve.wait_ge(s_xh, (EH + 1) * (i + 1))
                    if i == 0:
                        dve.wait_ge(s_half, 1)
                    for h in range(EH):
                        if k >= 1:
                            dve.wait_ge(s_tap, EH * ((DC - 1) * i + k - 1) + h + 1)
                        dve.scalar_tensor_tensor(xh[:, i % 2, h, back:L], xraw[:, h, 0:L - back],
                                                 Wh[:, h, k:k + 1], xh[:, i % 2, h, back:L],
                                                 ALU.mult, ALU.add).then_inc(s_tap, 1)
                elif task == "silu_u":
                    dve.wait_ge(s_tu, i + 1)
                    if i >= 2:
                        dve.wait_ge(s_uD, EH * (i - 1))
                    dve.scalar_tensor_tensor(u[:, i % 2], tu[:, :, :], 1.0, xh[:, i % 2], ALU.add,
                                             ALU.mult).then_inc(s_u, 1)
                elif task == "split":
                    dve.wait_ge(s_hi, i + 1)
                    m1, m2 = 2 * 2 * DS, 2 * DS
                    dve.tensor_tensor(rest1[:, :], xdbl[0:m1, :], parts[0:m1, i % 2, :], ALU.subtract).then_inc(s_rest, 1)
                    dve.wait_ge(s_rest, i + 1)
                    link(dve.tensor_copy(parts[0:m1, i % 2, :], rest1[:, :]))
                    link(dve.tensor_tensor(rest2[:, :], rest1[0:m2, :], parts[0:m2, i % 2, :], ALU.subtract))
                    dve.tensor_copy(parts[0:m2, i % 2, :], rest2[:, :]).then_inc(s_parts, 1)
                elif task == "delta":
                    dve.wait_ge(s_soft, 6 * i + 5)
                    link(dve.tensor_scalar(dy[:, :, :], dexp[:, :, :], 1.0, None, ALU.add))
                    link(dve.scalar_tensor_tensor(dnc[:, :, :], dy[:, :, :], -1.0, dexp[:, :, :], ALU.add, ALU.subtract))
                    link(dve.tensor_tensor(dsum[:, :, :], drel[:, :, :], dnc[:, :, :], ALU.subtract))
                    dve.wait_ge(s_soft, 6 * i + 6)
                    if i >= 2:
                        dve.wait_ge(s_dA, DS * (i - 1))
                        dve.wait_ge(s_dbu, DS * (i - 1))
                    dve.tensor_tensor(delta[:, i % 2], dln[:, :, :], dsum[:, :, :], ALU.add).then_inc(s_delta, 1)
                    dve.wait_ge(s_delta, i + 1)
                    dve.tensor_tensor(du[:, i % 2], delta[:, i % 2], u[:, i % 2], ALU.mult).then_inc(s_du, 1)
                elif task == "scan":
                    dve.wait_ge(s_dA, i + 1)
                    dve.wait_ge(s_dbu, i + 1)
                    if i >= 2:
                        dve.wait_ge(s_prod, i - 1)
                    flat = "p h l -> p (h l)"
                    dve.tensor_tensor_scan(hs[:, i % 2].rearrange(flat), psA[:, i % DA_RING].rearrange(flat),
                                           dbu[:, i % DBU_RING].rearrange(flat), 0.0, ALU.mult, ALU.add).then_inc(s_scan, 1)
                elif task == "prod":
                    dve.wait_ge(s_scan, i + 1)
                    dve.wait_ge(s_cps, i + 1)
                    if i >= PROD_RING:
                        dve.wait_ge(*added(i - PROD_RING))
                    dve.tensor_tensor(prod[:, i % PROD_RING], hs[:, i % 2], wide(psC[:, i % 2, 0:L], EH),
                                      ALU.mult).then_inc(s_prod, 1)
                elif task == "z_stats":
                    if i == 0:
                        dve.wait_ge(d_x0, 16)
                    if i == 1:
                        dve.wait_ge(d_x, 16 * (B - 1))
                    for h in range(LH):
                        dve.bn_stats(zst[:, i * LH + h, :], x_sb[:, i, h, :]).then_inc(s_zst, 1)
                    dve.wait_ge(s_zst, LH * (i + 1))
                    for h in range(LH):
                        dve.bn_aggr(zmv[:, i * LH + h, :], zst[:, i * LH + h, :]).then_inc(s_zmv, 1)
                elif task == "z_norm":
                    dve.wait_ge(s_zrs, i + 1)
                    dve.wait_ge(s_zmv, LH * (i + 1))
                    if i >= 1:
                        dve.wait_ge(s_zt, i)
                    for h in range(LH):
                        c = i * LH + h
                        dve.tensor_scalar(zn[:, h, :], x_sb[:, i, h, :], zmv[:, c, 0:1], zrs[:, c:c + 1],
                                          ALU.subtract, ALU.mult).then_inc(s_zn, 1)
                elif task == "z_gate":
                    dve.wait_ge(s_zt, i + 1)
                    dve.scalar_tensor_tensor(sz[:, i % 2], zt[:, :, :], 1.0, zn[:, :, :], ALU.add,
                                             ALU.mult).then_inc(s_sz, 1)
                elif task == "gate_y":
                    dve.wait_ge(s_sz, i + 1)
                    if i >= 1:
                        dve.wait_ge(s_yT, i)
                    if i == 0:
                        dve.wait_ge(*added(DS - 3))
                        dve.wait_ge(*added(DS - 1))
                        dve.tensor_tensor(ysum[:, :, :], psD[:, :, :], acc[:, 0], ALU.add).then_inc(s_ys, 1)
                        dve.wait_ge(s_ys, 1)
                        y = ysum[:, :, :]
                    else:
                        dve.wait_ge(*added(DS * (i + 1) - 1))
                        y = acc[:, i % 2]
                    dve.tensor_tensor(yg[:, :, :], y, sz[:, i % 2], ALU.mult).then_inc(s_yg, 1)
                elif task == "residual":
                    dve.wait_ge(s_yT, i + 1)
                    if i == 0:
                        dve.wait_ge(s_gates, 1)
                    dve.scalar_tensor_tensor(x2[:, i].rearrange("p h d -> p (h d)"), psM[:, :], gates[:, 0:1],
                                             x_sb[:, i].rearrange("p h d -> p (h d)"), ALU.mult, ALU.add).then_inc(s_x2, 1)
                    dve.wait_ge(s_x2, i + 1)
                    for h in range(LH):
                        dve.bn_stats(st2[:, h, :], x2[:, i, h, :]).then_inc(s_st2, 1)
                    dve.wait_ge(s_st2, LH * (i + 1))
                    if i >= 1:
                        dve.wait_ge(s_rs2, i)
                    for h in range(LH):
                        dve.bn_aggr(mv2[:, h, :], st2[:, h, :]).then_inc(s_mv2, 1)
                elif task == "norm":
                    dve.wait_ge(s_rs2, i + 1)
                    dve.wait_ge(s_mv2, LH * (i + 1))
                    if i >= 1:
                        dve.wait_ge(s_hT2, i)
                    for h in range(LH):
                        dve.tensor_scalar(hn[:, h, :], x2[:, i, h, :], mv2[:, h, 0:1], rs2[:, h:h + 1],
                                          ALU.subtract, ALU.mult).then_inc(s_hn, 1)
                elif task == "route":
                    dve.wait_ge(s_rex, i + 1)
                    link(dve.tensor_scalar(rs1[:, :], rex[:, :], 1.0, None, ALU.add))
                    link(dve.reciprocal(score[:, :], rs1[:, :]))
                    for h in range(LH):
                        last = dve.max(top[:, h, :], score[:, h * NE:(h + 1) * NE])
                    link(last)
                    for h in range(LH):
                        last = dve.max_index(topi[:, h, :], top[:, h, :], score[:, h * NE:(h + 1) * NE])
                    link(last)
                    dve.tensor_copy(topf[:, :, :], topi[:, :, 0:2])
                    link(dve.scalar_tensor_tensor(den[:, :], top[:, :, 0], 1e-20, top[:, :, 1], ALU.add, ALU.add))
                    link(dve.reciprocal(rden[:, :], den[:, :]))
                    link(dve.scalar_tensor_tensor(topw[:, :, :], top[:, :, 0:2], SCALE,
                                                  rden[:, :].unsqueeze(2).broadcast_to([P, LH, 2]), ALU.mult, ALU.mult))
                    for h in range(LH):
                        for r in range(2):
                            last = dve.tensor_scalar(pick[:, h, r, :], par[:, PC_IOTA:PC_IOTA + NE], topf[:, h, r:r + 1],
                                                     topw[:, h, r:r + 1], ALU.is_equal, ALU.mult)
                    link(last)
                    dve.tensor_tensor(wtok[:, i % 2], pick[:, :, 0, :], pick[:, :, 1, :], ALU.add).then_inc(s_w, 1)
                elif task == "mul":
                    mul(i)
                if task in ("gate", "flush"):
                    for unit in ([i] if task == "gate" else range(UNITS, UNITS + 4)):
                        if unit < UNITS:
                            dve.wait_ge(s_tanh, unit + 1)
                            dve.scalar_tensor_tensor(ag[:, unit % 2, :], tg[:, unit % 2, :], 1.0,
                                                     psU[:, unit % 2, 0:FF], ALU.add, ALU.mult).then_inc(s_ag, 1)
                        for g in groups_after(unit, 4):
                            t, q = divmod(g, NG)
                            if q == NG - 1:
                                b, lh = divmod(t, LH)
                                dve.wait_ge(s_dn, g + 1)
                                if t >= 2:
                                    dve.wait_ge(d_out[t % 2], 16 * (t // 2))
                                dve.scalar_tensor_tensor(outb[:, t % 2, :], psD[:, 0, :], gates[:, 1:2],
                                                         x2[:, b, lh, :], ALU.mult, ALU.add).then_inc(s_fin, 1)

        @block.gpsimd
        def _(pool):
            def times_b(m):
                b, n = divmod(m, DS)
                if n == 0:
                    pool.wait_ge(s_du, b + 1)
                if b == 0 and n % 2 == 0:
                    pool.wait_ge(s_bb, n // 2 + 1)
                if b >= 1 and n == 0:
                    pool.wait_ge(d_bb, 16 * b)
                if m >= DBU_RING:
                    pool.wait_ge(s_scan, m - DBU_RING + 1)
                pool.tensor_tensor(dbu[:, m % DBU_RING], du[:, b % 2], wide(bb[:, b % 2, n, :], EH),
                                   ALU.mult).then_inc(s_dbu, 1)

            for task, i in order:
                if task == "spread_b" and i == 0:
                    times_b(0)
                elif task == "scan":
                    if i + 1 < B * DS:
                        times_b(i + 1)
                elif task == "prod" and not on_pe(i):
                    b, n = divmod(i, DS)
                    pool.wait_ge(s_prod, i + 1)
                    if n == 0:
                        pool.wait_ge(s_uD, EH * (b + 1))
                        if b >= 2:
                            pool.wait_ge(s_yg, b - 1)
                        before = uD[:, b % 2]
                    else:
                        pool.wait_ge(*added(i - 2 if on_pe(i - 1) else i - 1))
                        before = acc[:, b % 2]
                    pool.tensor_tensor(acc[:, b % 2], before, prod[:, i % PROD_RING], ALU.add).then_inc(s_add, 1)
                elif task == "z_stats":
                    pool.wait_ge(s_zmv, LH * (i + 1))
                    if i == 0:
                        pool.wait_ge(s_mh, 1)
                    c = slice(i * LH, (i + 1) * LH)
                    pool.tensor_scalar(zve[:, c], zmv[:, c, 1], EPS, None, ALU.add).then_inc(s_zve, 1)
                    pool.wait_ge(s_zve, i + 1)
                    pool.tensor_tensor(zrs[:, c], zve[:, c], minus_half[:, c], ALU.pow).then_inc(s_zrs, 1)
                elif task == "residual":
                    pool.wait_ge(s_mv2, LH * (i + 1))
                    if i >= 1:
                        pool.wait_ge(s_hn, LH * i)
                    pool.tensor_scalar(ve2[:, :], mv2[:, :, 1], EPS, None, ALU.add).then_inc(s_ve2, 1)
                    pool.wait_ge(s_ve2, i + 1)
                    pool.tensor_tensor(rs2[:, :], ve2[:, :], minus_half[:, 0:LH], ALU.pow).then_inc(s_rs2, 1)


def kernel(**inputs):
    import concourse.bacc as bacc
    import ml_dtypes
    from concourse.bass_utils import run_bass_kernel_spmd

    a = {k: np.asarray(v) for k, v in inputs.items()}

    def halves(w):
        return w.reshape(w.shape[0], -1, P).transpose(2, 1, 0)

    def channels(w):
        return w.reshape(EH, P, -1).transpose(1, 0, 2).reshape(P, -1)

    params = np.concatenate([
        channels(a["L0_xattn_conv_w"]), channels(a["L0_xattn_conv_b"]), channels(a["L0_xattn_dt_proj_b"]),
        channels(a["L0_xattn_D"]), channels(a["L0_xattn_A_log"]),
        np.broadcast_to(a["g_xattn"].reshape(1, 1), (P, 1)), np.broadcast_to(a["g_ffn"].reshape(1, 1), (P, 1)),
        np.broadcast_to(np.arange(NE, dtype=np.float32), (P, NE))], axis=1)
    wx = a["L0_xattn_x_proj_w"]
    gate = np.concatenate([a["L0_ffn_shared_wg"].reshape(2, FF, D), a["L0_ffn_exp_wg"]])
    up = np.concatenate([a["L0_ffn_shared_wu"].reshape(2, FF, D), a["L0_ffn_exp_wu"]])
    both = np.concatenate([gate, up], axis=1)
    rows = np.arange(XROWS) % (2 * DS)
    arrays = {
        "ctxT": a["ctx_1024"].transpose(2, 0, 1),
        "x": a["x"],
        "params": params,
        "w_in": a["L0_xattn_in_proj_w"].T,
        "w_x": halves(np.concatenate([wx[DR:], wx[DR:], wx[DR:], wx[:DR]])),
        "w_dt": a["L0_xattn_dt_proj_w"].T,
        "w_gate": halves(a["L0_ffn_gate_w"]),
        "w_up": both.reshape(NU, 2 * FF, KT, P).transpose(3, 2, 0, 1),
        "w_down": np.concatenate([a["L0_ffn_shared_wd"].T, a["L0_ffn_exp_wd"].transpose(0, 2, 1).reshape(NE * FF, D)]),
        "ident": np.eye(P, dtype=np.float32),
        "sel": np.broadcast_to((rows[:, None] == np.arange(2 * DS))[:, :, None], (XROWS, 2 * DS, P)).astype(ml_dtypes.bfloat16),
    }
    arrays = {f"in_{k}": np.ascontiguousarray(v) for k, v in arrays.items()}
    nc = bacc.Bacc("TRN2", target_bir_lowering=False, num_devices=1)
    args = [nc.dram_tensor(k, v.shape, mybir.dt.from_np(v.dtype), kind="ExternalInput").ap() for k, v in arrays.items()]
    out = nc.dram_tensor("out_0", (B, L, D), F32, kind="ExternalOutput").ap()
    mixer(nc, *args, out)
    return run_bass_kernel_spmd(nc, [arrays], core_ids=[0]).results[0]["out_0"]
```

```python
from contextlib import ExitStack

import numpy as np

import concourse.bass as bass
from concourse import mybir

F32 = mybir.dt.float32
BF16 = mybir.dt.bfloat16
F32R = mybir.dt.float32r
U32 = mybir.dt.uint32
ALU = mybir.AluOpType
ACT = mybir.ActivationFunctionType

P = 128
B, L, D = 4, 256, 256
DM, DI, DS, DC, DR = 128, 256, 16, 4, 8
EH = DI // P
LH = L // P
KT = D // P
NE, FF = 8, 176
NU = NE + 2
FCAT = NU * FF
FB = (FCAT + P - 1) // P
LASTF = FCAT - (FB - 1) * P
SCALE = 2.5
EPS = 1e-5

PC_CONVW = 0
PC_CONVB = PC_CONVW + EH * DC
PC_DTB = PC_CONVB + EH
PC_D = PC_DTB + EH
PC_ALOG = PC_D + EH
PC_GX = PC_ALOG + EH * DS
PC_GF = PC_GX + 1
PC_IOTA = PC_GF + 1
NPC = PC_IOTA + NE

XROWS = 3 * 2 * DS
XM = XROWS + DR

WARM = (6, 20, 1, 6)
PE_STATES = 8
DA_RING, DBU_RING, PROD_RING, HT_RING = 2, 3, 3, 3

STEPS = B * DS
NS = LH
HALF = DS // NS
W = NS * EH * P
TILES = B * LH

UNITS = B * LH * NU
NSPLIT = NU // 2
GROUPS = [(0, 4), (4, 8), (8, 12), (12, FB)]
NG = len(GROUPS)


def group_last_unit(g):
    return (min(GROUPS[g][1] * P, FCAT) - 1) // FF


def part_end(p):
    return (p + 1) * HALF


def step_range(m):
    b, n = divmod(m, DS)
    half, k = divmod(n, HALF)
    return b, NS * k, half * P, (half + 1) * P


AT = {"spread_c": 0.669, "carry_in": 0, "scan": 0.39, "prod": 1.713}
BEFORE = {"project": 3.496, "project_out": 4.382, "tap0": 4.519, "tap1": 5.199, "tap2": 7.081, "tanh_u": 7.435,
          "silu_u": 7.735, "xproj": 7.802, "xproj_out": 8.529, "split0": 8.98, "dt": 9.501, "dt_out": 10.143,
          "relu_out": 10.349, "split1": 10.395, "split2": 10.82, "soft_exp": 10.866, "soft_log": 11.116,
          "split3": 11.16, "log_1": 11.882, "log_2": 12.281, "delta0": 12.485, "delta1": 13.151, "delta2": 13.574,
          "edge_in": 13.869, "edge_out": 15.045}
SHIFT = (0, 0.019, -0.078, -0.07)
BEHIND = {"skip": -0.408, "gate_y": 1.726, "to_tokens": 2.226, "residual": 2.843, "stats": 3.129, "variance": 3.347,
          "norm": 3.99, "to_features": 4.27, "to_features_out": 4.937, "features_hi": 4.947, "features_lo": 4.989,
          "logits": 4.994, "logits_out": 5.188, "route0": 5.583, "route1": 5.819, "route2": 5.855, "route3": 6.075,
          "route4": 6.556, "route5": 6.721, "route6": 6.939}
CHAIN_FROM = 1.3
CHAIN = (1.003, 1.144, 0.937, 1.145, 0.93, 1.152, 1.157, 1.225)
GATE = {"z_stats": 1.097, "z_norm": 4.198, "z_gate": 5.954}
WEIGHTS_FROM, WEIGHTS_EVERY = 4, 1.5
UNIT = {"up": 0, "gate": 0.026, "mul": 0.302, "hidden": 0.321}
SHARED_FROM, ROUTED_FROM = 5, -0.3
UNITS_PER_STEP = (1.149, 1.248, 1.248, 1.252, 1.248, 1.234, 1.199, 0.916)


def unit_times():
    at = []
    for unit in range(UNITS):
        t, j = divmod(unit, NU)
        time = part_end(t) + CHAIN_FROM + (SHARED_FROM - CHAIN_FROM if j < 2 else ROUTED_FROM - CHAIN_FROM) * CHAIN[t]
        if at:
            time = max(time, at[-1] + 1 / UNITS_PER_STEP[t])
        at.append(time)
    return at


def schedule():
    times = [(m + AT[task], task, m) for m in range(STEPS) for task in ("spread_c", "scan", "prod")]
    times += [(m + AT["carry_in"], "carry_in", m) for m in range(STEPS) if m % DS >= HALF]
    times += [(DS * (b - 1) + at + SHIFT[b], task, b) for b in range(1, B) for task, at in BEFORE.items()]
    times += [(DS * b + at, task, b) for b in range(B) for task, at in GATE.items()]
    times += [(part_end(p) + CHAIN_FROM + (at - CHAIN_FROM) * CHAIN[p], task, p) for p in range(TILES)
              for task, at in BEHIND.items()]
    times += [(WEIGHTS_FROM + WEIGHTS_EVERY * k + late, task, k) for k in range(NSPLIT)
              for late, task in ((0.0, "weights_hi"), (0.6, "weights_lo"))]
    at = unit_times()
    for unit in range(UNITS):
        times += [(at[unit] + UNIT[task], task, unit) for task in ("up", "hidden")]
        after = at[min(unit + 1, UNITS - 1)] + (unit + 1 == UNITS)
        times += [(after + UNIT[task], task, unit) for task in ("gate", "mul")]
    prologue = [(task, 0) for task in (
        "load", "project", "project_out", "tap0", "tap1", "tap2", "tanh_u", "silu_u", "xproj", "xproj_out", "split0",
        "split1", "split2", "split3", "dt", "dt_out", "soft_exp", "relu_out", "soft_log")]
    prologue += [("spread_b", 0), ("spread_b", 1)]
    prologue += [(task, 0) for task in ("log_1", "log_2", "delta0", "delta1", "delta2", "first", "edge_in",
                                        "edge_out")]
    return prologue + [(task, i) for time, task, i in sorted(times)] + [("flush", UNITS)]


def mixer(nc, ctxT, x, params, w_in, w_x, w_dt, w_gate, w_up, w_down, ident_in, sel_in, out):
    order = schedule()
    with ExitStack() as stack:
        def sb(name, shape, dt=F32):
            return stack.enter_context(nc.sbuf_tensor(name, shape, dt))

        def ps(name, shape, dt=F32):
            return stack.enter_context(nc.psum_tensor(name, shape, dt))

        def sem(name):
            return stack.enter_context(nc.semaphore(name))

        ctx_sb = sb("ctx_sb", [P, B, L])
        x_sb = sb("x_sb", [P, B, LH, D])
        par = sb("par", [P, NPC])
        win = sb("win", [P, DI])
        wx = sb("wx", [P, EH, XM])
        wdt = sb("wdt", [P, DI])
        wg = sb("wg", [P, KT, NE])
        wup = sb("wup", [P, NU - NSPLIT, KT, 2 * FF])
        whi = sb("whi", [P, NSPLIT, KT, 2 * FF], F32R)
        wlo = sb("wlo", [P, NSPLIT, KT, 2 * FF], F32R)
        wdn = sb("wdn", [P, FB, D])
        ident = sb("ident", [P, P])
        sel = sb("sel", [P, 2 * DS, P], BF16)
        zeros = sb("zeros", [P, 512], BF16)
        cwh = sb("cwh", [P, EH * DC + EH])
        aneg = sb("aneg", [P, EH * DS])
        aexp = sb("aexp", [P, EH * DS])
        gtanh = sb("gtanh", [P, 2])
        gates = sb("gates", [P, 2])
        minus_half = sb("minus_half", [P, B * LH])
        zst = sb("zst", [P, B * LH, 6])
        zmv = sb("zmv", [P, B * LH, 2])
        zve = sb("zve", [P, B * LH])
        zrs = sb("zrs", [P, B * LH])
        zn = sb("zn", [P, LH, L])
        zt = sb("zt", [P, LH, L])
        sz = sb("sz", [P, LH, L])
        xh = sb("xh", [P, EH, L])
        u = sb("u", [P, 2, EH, L])
        xdbl = sb("xdbl", [P, L])
        parts = sb("parts", [XROWS, 2, L], BF16)
        rest1 = sb("rest1", [2 * 2 * DS, L])
        rest2 = sb("rest2", [2 * DS, L])
        dabs = sb("dabs", [P, EH, L])
        dln = sb("dln", [P, EH, L])
        drel = sb("drel", [P, EH, L])
        dy = sb("dy", [P, EH, L])
        dnc = sb("dnc", [P, EH, L])
        dexp, dsum, xraw, tu = dabs, dnc, dy, drel
        delta = sb("delta", [P, 2, EH, L])
        du = sb("du", [P, 2, EH, L])
        uD = sb("uD", [P, EH, P])
        bb = sb("bb", [P, 2, DS, L])
        dbu = sb("dbu", [P, DBU_RING, W])
        hs = sb("hs", [P, 2, W])
        prod = sb("prod", [P, PROD_RING, W])
        acc = sb("acc", [P, 2, W])
        eraw = sb("eraw", [P, EH, DS])
        edge = sb("edge", [P, EH, DS])
        carry = sb("carry", [P, HALF, LH * EH])
        ysum = sb("ysum", [P, EH, P])
        yg = sb("yg", [P, EH, L])
        x2 = x_sb
        st2 = sb("st2", [P, LH, 6])
        mv2 = sb("mv2", [P, LH, 2])
        ve2 = sb("ve2", [P, LH])
        rs2 = sb("rs2", [P, LH])
        hn = sb("hn", [P, LH, D])
        hnT = sb("hnT", [P, 2, KT, L])
        hnhi = sb("hnhi", [P, 2, KT, P], F32R)
        hnlo = sb("hnlo", [P, 2, KT, P], F32R)
        rex = sb("rex", [P, LH * NE])
        rs1 = sb("rs1", [P, LH * NE])
        score = sb("score", [P, LH * NE])
        top = sb("top", [P, LH, 8])
        topi = sb("topi", [P, LH, 8], U32)
        topf = sb("topf", [P, LH, 2])
        den = sb("den", [P, LH])
        rden = sb("rden", [P, LH])
        topw = sb("topw", [P, LH, 2])
        pick = sb("pick", [P, LH, 2, NE])
        wtok = sb("wtok", [P, 2, LH, NE])
        tg = sb("tg", [P, 2, FF])
        ag = sb("ag", [P, 2, FF])
        hcat = sb("hcat", [P, 2, FCAT])
        hT = sb("hT", [P, HT_RING, 4 * P])
        outb = sb("outb", [P, 2, D])

        brows = nc.dram_tensor("brows", (B, DS, L), F32).ap()

        psA = ps("psA", [P, DA_RING, W])
        psC = ps("psC", [P, 2, 512])
        psM = ps("psM", [P, 512])
        psU = ps("psU", [P, 2, 512])
        psD = ps("psD", [P, 2, D])

        d_par, d_ctx0, d_ctx, d_win, d_wx = sem("d_par"), sem("d_ctx0"), sem("d_ctx"), sem("d_win"), sem("d_wx")
        d_wdt, d_id, d_sel, d_x0, d_x = sem("d_wdt"), sem("d_id"), sem("d_sel"), sem("d_x0"), sem("d_x")
        d_wg, d_wup, d_wdn, d_wst = sem("d_wg"), sem("d_wup"), sem("d_wdn"), sem("d_wst")
        s_whi, s_wlo, s_hnhi, s_hnlo = sem("s_whi"), sem("s_wlo"), sem("s_hnhi"), sem("s_hnlo")
        d_brow, d_bb = sem("d_brow"), sem("d_bb")
        d_out = [sem("d_out0"), sem("d_out1")]
        s_half, s_aexp, s_aneg, s_gt, s_gates = sem("s_half"), sem("s_aexp"), sem("s_aneg"), sem("s_gt"), sem("s_gates")
        s_mh, s_zero = sem("s_mh"), sem("s_zero")
        s_blank = sem("s_blank")
        s_edge, s_edge_dA, s_fix = sem("s_edge"), sem("s_edge_dA"), sem("s_fix")
        s_zst, s_zmv, s_zve, s_zrs, s_zn, s_zt, s_sz = (sem("s_zst"), sem("s_zmv"), sem("s_zve"), sem("s_zrs"),
                                                       sem("s_zn"), sem("s_zt"), sem("s_sz"))
        s_xin, s_xh, s_tap, s_tu, s_u = sem("s_xin"), sem("s_xh"), sem("s_tap"), sem("s_tu"), sem("s_u")
        s_xdbl, s_xd, s_hi, s_rest, s_parts = sem("s_xdbl"), sem("s_xd"), sem("s_hi"), sem("s_rest"), sem("s_parts")
        s_dtp, s_abs, s_dnc, s_del = sem("s_dtp"), sem("s_abs"), sem("s_dnc"), sem("s_del")
        s_delta, s_du, s_uD = sem("s_delta"), sem("s_du"), sem("s_uD")
        s_relu, s_exp, s_ln = sem("s_relu"), sem("s_exp"), sem("s_ln")
        s_bps, s_bb, s_cps, s_dA, s_dbu = sem("s_bps"), sem("s_bb"), sem("s_cps"), sem("s_dA"), sem("s_dbu")
        s_scan, s_prod, s_add, s_nsum, s_carry = (sem("s_scan"), sem("s_prod"), sem("s_add"), sem("s_nsum"),
                                                     sem("s_carry"))
        s_y2 = sem("s_y2")
        s_ys, s_yg, s_yT, s_x2, s_st2, s_mv2, s_ve2, s_rs2 = (sem("s_ys"), sem("s_yg"), sem("s_yT"), sem("s_x2"),
                                                             sem("s_st2"), sem("s_mv2"), sem("s_ve2"), sem("s_rs2"))
        s_hn, s_hT2, s_hnT, s_log, s_rex, s_w = (sem("s_hn"), sem("s_hT2"), sem("s_hnT"), sem("s_log"),
                                                       sem("s_rex"), sem("s_w"))
        s_up, s_tanh, s_ag, s_mul, s_tr, s_ht, s_dn, s_fin = (sem("s_up"), sem("s_tanh"), sem("s_ag"), sem("s_mul"),
                                                             sem("s_tr"), sem("s_ht"), sem("s_dn"), sem("s_fin"))
        s_chain = sem("s_chain")

        staged = hcat.rearrange("p t c -> p (t c)").rearrange("p (u k f) -> p u k f", u=NSPLIT, k=KT)
        Wh = cwh[:, 0:EH * DC].rearrange("p (h k) -> p h k", h=EH)

        def tile(ap):
            return ap.rearrange("p (s h l) -> p s h l", s=NS, h=EH)

        def on_pe(m):
            return m < part_end(0)

        def added(m):
            if on_pe(m):
                return s_nsum, m + 1
            part, k = divmod(m - HALF, HALF)
            return s_add, (HALF - 1) * part + max(k, 1)

        def fixes(m):
            return HALF * (m // DS) + m % HALF + 1

        def groups_after(unit, lag):
            u0 = unit - lag
            if u0 < 0 or u0 >= UNITS:
                return []
            t, j = divmod(u0, NU)
            return [NG * t + g for g in range(NG) if group_last_unit(g) == j]

        def finish_delta(engine, task, i):
            if task == "delta0":
                engine.wait_ge(s_dnc, i + 1)
                engine.wait_ge(s_relu, i + 1)
                engine.tensor_tensor(dsum[:, :, :], drel[:, :, :], dnc[:, :, :], ALU.subtract).then_inc(s_del, 1)
            elif task == "delta1":
                engine.wait_ge(s_del, i + 1)
                engine.wait_ge(s_ln, i + 1)
                if i >= 2:
                    engine.wait_ge(s_dA, DS * (i - 1))
                    engine.wait_ge(s_dbu, DS * (i - 1))
                engine.tensor_tensor(delta[:, i % 2], dln[:, :, :], dsum[:, :, :], ALU.add).then_inc(s_delta, 1)
            else:
                engine.wait_ge(s_delta, i + 1)
                engine.wait_ge(s_u, i + 1)
                engine.tensor_tensor(du[:, i % 2], delta[:, i % 2], u[:, i % 2], ALU.mult).then_inc(s_du, 1)

        block = stack.enter_context(nc.Block())

        @block.sync
        def _(sp):
            sp.dma_start(ctx_sb[:, 0, :], ctxT[:, 0, :]).then_inc(d_ctx0, 16)
            sp.dma_start(wx[:, :, :], w_x).then_inc(d_wx, 16)
            sp.dma_start(wdt[XROWS:XM, :], w_dt).then_inc(d_wdt, 16)
            sp.dma_start(sel[0:XROWS, :, :], sel_in).then_inc(d_sel, 16)
            sp.dma_start(ident[:, :], ident_in).then_inc(d_id, 16)
            sp.dma_start(x_sb[:, 0], x[0].rearrange("(h p) d -> p h d", p=P)).then_inc(d_x0, 16)
            sp.dma_start(ctx_sb[:, 1:B, :], ctxT[:, 1:B, :]).then_inc(d_ctx, 16)
            for b in range(1, B):
                sp.dma_start(x_sb[:, b], x[b].rearrange("(h p) d -> p h d", p=P)).then_inc(d_x, 16)
            for task, i in order:
                if task == "xproj":
                    sp.wait_ge(s_xd, i + 1)
                    sp.dma_start(brows[i], xdbl[0:DS, :]).then_inc(d_brow, 16)
                elif task == "dt":
                    sp.wait_ge(d_brow, 16 * (i + 1))
                    if i == 0:
                        for n0, n1, l0 in ((PE_STATES, DS, 0), (0, PE_STATES, P)):
                            sp.dma_start(bb[:, 0, n0:n1, l0:L], brows[0, n0:n1, l0:L].unsqueeze(0).broadcast_to(
                                [P, n1 - n0, L - l0])).then_inc(d_bb, 16)
                        sp.dma_start(wg[:, :, :], w_gate).then_inc(d_wg, 16)
                        for k in range(KT):
                            sp.dma_start(staged[:, :, k], w_up[:, 1::2, k]).then_inc(d_wst, 16)
                        for k in range(KT):
                            sp.dma_start(wup[:, :, k], w_up[:, 0::2, k]).then_inc(d_wup, 16)
                        sp.dma_start(wdn[:, 0:FB - 1, :],
                                     w_down[0:(FB - 1) * P].rearrange("(f p) d -> p f d", p=P)).then_inc(d_wdn, 16)
                        sp.dma_start(wdn[0:LASTF, FB - 1, :], w_down[(FB - 1) * P:FCAT]).then_inc(d_wdn, 16)
                    else:
                        if i >= 2:
                            sp.wait_ge(s_dbu, DS * (i - 1))
                        sp.dma_start(bb[:, i % 2], brows[i].unsqueeze(0).broadcast_to([P, DS, L])).then_inc(d_bb, 16)
                elif task in ("hidden", "flush"):
                    for unit in ([i] if task == "hidden" else range(UNITS, UNITS + 4)):
                        for g in groups_after(unit, 4):
                            t, q = divmod(g, NG)
                            if q == NG - 1:
                                b, h = divmod(t, LH)
                                sp.wait_ge(s_fin, t + 1)
                                sp.dma_start(out[b, h * P:(h + 1) * P, :], outb[:, t % 2, :]).then_inc(d_out[t % 2], 16)
            for q in d_out:
                sp.wait_ge(q, 16 * B * LH // 2)

        @block.tensor
        def _(pe):
            psM_read = []

            def take_misc(reader, value):
                if psM_read:
                    pe.wait_ge(*psM_read.pop())
                psM_read.append((reader, value))

            def spread_b(k):
                pe.wait_ge(s_parts, 1)
                for i in range(4):
                    last = pe.matmul(psU[:, k, i * P:(i + 1) * P], sel[0:XROWS, 4 * k + i, :], parts[:, 0, 0:P],
                                     start=True, stop=True)
                last.then_inc(s_bps, 1)

            def keep_warm(n):
                for _ in range(n):
                    pe.matmul(psC[:, 0, :], zeros[:, 0:P], zeros[:, :], start=True, stop=True)

            pe.wait_ge(s_blank, 1)
            keep_warm(WARM[0])
            for task, i in order:
                if i == 0 and task in ("xproj", "dt", "spread_b"):
                    keep_warm(WARM[("project", "xproj", "dt", "spread_b").index(task)])
                if task == "project":
                    take_misc(s_xh, (EH + 1) * (i + 1))
                    if i == 0:
                        pe.wait_ge(d_ctx0, 16)
                        pe.wait_ge(d_win, 16)
                    if i == 1:
                        pe.wait_ge(d_ctx, 16)
                    for h in range(EH):
                        last = pe.matmul(psM[:, h * L:(h + 1) * L], win[:, h * P:(h + 1) * P], ctx_sb[:, i, :],
                                         start=True, stop=True)
                    last.then_inc(s_xin, 1)
                elif task == "xproj":
                    take_misc(s_xd, i + 1)
                    if i == 0:
                        pe.wait_ge(d_wx, 16)
                    pe.wait_ge(s_u, i + 1)
                    for h in range(EH):
                        last = pe.matmul(psM[0:XM, 0:L], wx[:, h, :], u[:, i % 2, h, :], start=(h == 0), stop=(h == EH - 1))
                    last.then_inc(s_xdbl, 1)
                elif task == "dt":
                    take_misc(s_relu, i + 1)
                    if i == 0:
                        pe.wait_ge(d_wdt, 16)
                    pe.wait_ge(s_xd, i + 1)
                    for h in range(EH):
                        last = pe.matmul(psM[:, h * L:(h + 1) * L], wdt[XROWS:XM, h * P:(h + 1) * P],
                                         xdbl[XROWS:XM, :], start=True, stop=True)
                    last.then_inc(s_dtp, 1)
                elif task == "spread_b":
                    if i == 0:
                        pe.wait_ge(d_sel, 16)
                    spread_b(i)
                elif task == "spread_c":
                    b, s0, l0, l1 = step_range(i)
                    if i == 0:
                        pe.wait_ge(d_sel, 16)
                    if i % DS == 0:
                        pe.wait_ge(s_parts, b + 1)
                    if i >= 2:
                        pe.wait_ge(s_prod, i - 1)
                    for j in range(NS):
                        last = pe.matmul(psC[:, i % 2, j * P:(j + 1) * P], sel[0:XROWS, DS + s0 + j, :],
                                         parts[:, b % 2, l0:l1], start=True, stop=True)
                    last.then_inc(s_cps, 1)
                elif task == "prod" and on_pe(i):
                    if i == 0:
                        pe.wait_ge(d_id, 16)
                    pe.wait_ge(s_prod, i + 1)
                    for j in range(LH):
                        last = pe.matmul(psD[:, 0, :], ident[:, :], prod[:, i % PROD_RING, j * EH * P:(j + 1) * EH * P],
                                         start=(i == 0 and j == 0), stop=(i == part_end(0) - 1 and j == LH - 1))
                    last.then_inc(s_nsum, 1)
                elif task == "to_tokens":
                    take_misc(s_x2, i + 1)
                    pe.wait_ge(s_yg, i + 1)
                    b, lh = divmod(i, LH)
                    for h in range(EH):
                        last = pe.transpose(psM[:, lh * D + h * P:lh * D + (h + 1) * P],
                                            yg[:, h, lh * P:(lh + 1) * P], ident[:, :])
                    last.then_inc(s_yT, 1)
                elif task == "to_features":
                    take_misc(s_hnT, i + 1)
                    pe.wait_ge(s_hn, i + 1)
                    lh = i % LH
                    for k in range(KT):
                        last = pe.transpose(psM[:, k * L + lh * P:k * L + (lh + 1) * P],
                                            hn[:, lh, k * P:(k + 1) * P], ident[:, :])
                    last.then_inc(s_hT2, 1)
                elif task == "logits":
                    take_misc(s_rex, i + 1)
                    if i == 0:
                        pe.wait_ge(d_wg, 16)
                    pe.wait_ge(s_hnT, i + 1)
                    b, lh = divmod(i, LH)
                    for k in range(KT):
                        last = pe.matmul(psM[:, lh * NE:(lh + 1) * NE], hnT[:, b % 2, k, lh * P:(lh + 1) * P],
                                         wg[:, k, :], start=(k == 0), stop=(k == KT - 1))
                    last.then_inc(s_log, 1)
                if task in ("up", "flush"):
                    for unit in ([i] if task == "up" else range(UNITS, UNITS + 4)):
                        for g in groups_after(unit, 2):
                            t, q = divmod(g, NG)
                            take_misc(s_ht, g + 1)
                            pe.wait_ge(s_mul, unit - 1)
                            for f in range(*GROUPS[q]):
                                m = P if f < FB - 1 else LASTF
                                c = (f - GROUPS[q][0]) * P
                                last = pe.transpose(psM[0:m, c:c + P], hcat[:, t % 2, f * P:f * P + m], ident[:, :])
                            last.then_inc(s_tr, 1)
                        if unit < UNITS:
                            t, j = divmod(unit, NU)
                            b, lh = divmod(t, LH)
                            if unit == 0:
                                pe.wait_ge(d_wup, 16 * KT)
                            if j == 0:
                                pe.wait_ge(s_hnT, t + 1)
                            if unit >= 2:
                                pe.wait_ge(s_mul, unit - 1)
                            else:
                                pe.wait_ge(s_bb, unit + 1)
                            dst = psU[:, unit % 2, 0:2 * FF]
                            if j % 2 == 0:
                                for k in range(KT):
                                    last = pe.matmul(dst, hnT[:, b % 2, k, lh * P:(lh + 1) * P], wup[:, j // 2, k, :],
                                                     start=(k == 0), stop=(k == KT - 1))
                            else:
                                if unit == 1:
                                    pe.wait_ge(s_wlo, NSPLIT)
                                if j == 1:
                                    pe.wait_ge(s_hnlo, t + 1)
                                for k in range(KT):
                                    h_hi, h_lo = hnhi[:, t % 2, k, :], hnlo[:, t % 2, k, :]
                                    w_hi, w_lo = whi[:, j // 2, k, :], wlo[:, j // 2, k, :]
                                    pe.matmul(dst, h_hi, w_hi, start=(k == 0), stop=False)
                                    pe.matmul(dst, h_hi, w_lo, start=False, stop=False)
                                    last = pe.matmul(dst, h_lo, w_hi, start=False, stop=(k == KT - 1))
                            last.then_inc(s_up, 1)
                        for g in groups_after(unit, 3):
                            t, q = divmod(g, NG)
                            if g == 0:
                                pe.wait_ge(d_wdn, 32)
                            if q == 0 and t >= 1:
                                pe.wait_ge(s_fin, t)
                            if q == 0 and t == 0:
                                pe.wait_ge(s_ys, 1)
                            pe.wait_ge(s_ht, g + 1)
                            for f in range(*GROUPS[q]):
                                m = P if f < FB - 1 else LASTF
                                c = (f - GROUPS[q][0]) * P
                                last = pe.matmul(psD[:, 0, :], hT[0:m, g % HT_RING, c:c + P], wdn[0:m, f, :],
                                                 start=(f == 0), stop=(f == FB - 1))
                            last.then_inc(s_dn, 1)

        @block.scalar
        def _(act):
            act.dma_start(win[:, :], w_in).then_inc(d_win, 16)
            act.dma_start(par[:, :], params).then_inc(d_par, 16)

            def exps(m):
                b, s0, l0, l1 = step_range(m)
                if m % DS == 0:
                    act.wait_ge(s_delta, b + 1)
                if m == 0:
                    act.wait_ge(s_aneg, 1)
                if m == 0:
                    act.wait_ge(s_zero, 1)
                if m >= DA_RING:
                    act.wait_ge(s_scan, m - DA_RING + 1)
                dst = tile(psA[:, m % DA_RING])
                for j in range(NS):
                    for h in range(EH):
                        last = act.activation(dst[:, j, h, 1:], delta[:, b % 2, h, l0 + 1:l1], ACT.Exp,
                                              scale=aneg[:, h * DS + s0 + j:h * DS + s0 + j + 1])
                last.then_inc(s_dA, 1)

            def copy_b(k):
                act.wait_ge(s_bps, k + 1)
                act.copy(bb[:, 0, 4 * k:4 * k + 4, 0:P], psU[:, k].rearrange("p (s l) -> p s l", l=P)).then_inc(s_bb, 1)

            for task, i in order:
                if task == "load":
                    act.preload_act_table_set("exp_and_others")
                    act.wait_ge(d_par, 16)
                    act.activation(gtanh[:, :], par[:, PC_GX:PC_GX + 2], ACT.Tanh).then_inc(s_gt, 1)
                    act.activation(aexp[:, :], par[:, PC_ALOG:PC_ALOG + EH * DS], ACT.Exp).then_inc(s_aexp, 1)
                elif task == "project_out":
                    act.wait_ge(s_xin, i + 1)
                    if i == 0:
                        act.wait_ge(s_half, 1)
                    else:
                        act.wait_ge(s_u, i)
                    for h in range(EH):
                        act.activation(xh[:, h, :], psM[:, h * L:(h + 1) * L], ACT.Identity,
                                       scale=Wh[:, h, DC - 1:DC],
                                       bias=cwh[:, EH * DC + h:EH * DC + h + 1]).then_inc(s_xh, 1)
                    if i >= 1:
                        act.wait_ge(s_dnc, i)
                    act.copy(xraw[:, :, :].rearrange("p h l -> p (h l)"), psM[:, :]).then_inc(s_xh, 1)
                elif task == "tanh_u":
                    act.wait_ge(s_tap, EH * (DC - 1) * (i + 1))
                    if i >= 1:
                        act.wait_ge(s_del, i)
                    act.activation(tu[:, :, :], xh[:, :, :], ACT.Tanh).then_inc(s_tu, 1)
                    if i == 0:
                        act.preload_act_table_set("natural_log_exp_and_others")
                elif task == "xproj_out":
                    act.wait_ge(s_xdbl, i + 1)
                    if i >= 1:
                        act.wait_ge(s_dtp, i)
                        act.wait_ge(s_rest, i)
                    if i >= 1:
                        act.wait_ge(d_brow, 16 * i)
                    act.copy(xdbl[0:XM, :], psM[0:XM, 0:L]).then_inc(s_xd, 1)
                    if i >= 2:
                        act.wait_ge(s_cps, DS * (i - 1))
                    if i == 2:
                        act.wait_ge(s_bps, PE_STATES // 4)
                    act.wait_ge(s_xd, i + 1)
                    act.copy(parts[:, i % 2, :], xdbl[0:XROWS, :]).then_inc(s_hi, 1)
                elif task == "dt_out":
                    act.wait_ge(s_dtp, i + 1)
                    if i >= 1:
                        act.wait_ge(s_delta, i)
                    for h in range(EH):
                        last = act.activation(dabs[:, h, :], psM[:, h * L:(h + 1) * L], ACT.Abs,
                                              bias=par[:, PC_DTB + h:PC_DTB + h + 1])
                    last.then_inc(s_abs, 1)
                elif task == "relu_out":
                    act.wait_ge(s_u, i + 1)
                    for h in range(EH):
                        last = act.activation(drel[:, h, :], psM[:, h * L:(h + 1) * L], ACT.Relu,
                                              bias=par[:, PC_DTB + h:PC_DTB + h + 1])
                    last.then_inc(s_relu, 1)
                elif task == "soft_exp":
                    if i >= 1:
                        act.preload_act_table_set("natural_log_exp_and_others")
                    act.wait_ge(s_abs, i + 1)
                    act.activation(dexp[:, :, :], dabs[:, :, :], ACT.Exp, scale=-1.0).then_inc(s_exp, 1)
                elif task == "soft_log":
                    act.wait_ge(s_exp, i + 1)
                    act.activation(dln[:, :, :], dexp[:, :, :], ACT.Ln, bias=1.0).then_inc(s_ln, 1)
                elif task == "skip":
                    b, half = divmod(i, LH)
                    act.wait_ge(s_u, b + 1)
                    if i >= 1:
                        act.wait_ge(s_ys, i)
                    for h in range(EH):
                        last = act.activation(uD[:, h, :], u[:, b % 2, h, half * P:(half + 1) * P], ACT.Copy,
                                              scale=par[:, PC_D + h:PC_D + h + 1])
                    last.then_inc(s_uD, 1)
                elif task == "spread_b":
                    copy_b(i)
                elif task == "edge_out":
                    act.wait_ge(s_edge, i + 1)
                    if i >= 1:
                        act.wait_ge(s_carry, HALF * i)
                    act.activation(edge[:, :, :], eraw[:, :, :], ACT.Exp).then_inc(s_edge_dA, 1)
                elif task == "first":
                    exps(0)
                elif task == "scan":
                    if i + 1 < B * DS:
                        exps(i + 1)
                elif task == "z_gate":
                    act.wait_ge(s_zn, LH * (i + 1))
                    if i >= 1:
                        act.wait_ge(s_sz, i)
                    act.activation(zt[:, :, :], zn[:, :, :], ACT.Tanh, scale=0.5).then_inc(s_zt, 1)
                elif task == "to_features_out":
                    b, h = divmod(i, LH)
                    act.wait_ge(s_hT2, i + 1)
                    if b >= 2:
                        act.wait_ge(s_up, LH * NU * (b - 1))
                    c = slice(h * P, (h + 1) * P)
                    act.copy(hnT[:, b % 2, :, c], psM.rearrange("p (k l) -> p k l", k=KT)[:, :, c]).then_inc(s_hnT, 1)
                elif task == "features_hi":
                    b, h = divmod(i, LH)
                    act.wait_ge(s_hnT, i + 1)
                    if i >= 2:
                        act.wait_ge(s_up, NU * (i - 1))
                    act.copy(hnhi[:, i % 2], hnT[:, b % 2, :, h * P:(h + 1) * P]).then_inc(s_hnhi, 1)
                elif task == "weights_hi":
                    if i == 0:
                        act.wait_ge(d_wst, 16 * KT)
                    act.copy(whi[:, i], staged[:, i]).then_inc(s_whi, 1)
                elif task == "logits_out":
                    act.wait_ge(s_log, i + 1)
                    if i >= 1:
                        act.wait_ge(s_w, i)
                    c = slice(i % LH * NE, (i % LH + 1) * NE)
                    act.activation(rex[:, c], psM[:, c], ACT.Exp, scale=-1.0).then_inc(s_rex, 1)
                elif task == "gate":
                    act.wait_ge(s_up, i + 1)
                    if i >= 2:
                        act.wait_ge(s_ag, i - 1)
                    act.activation(tg[:, i % 2, :], psU[:, i % 2, 0:FF], ACT.Tanh, scale=0.5).then_inc(s_tanh, 1)
                if task in ("hidden", "flush"):
                    for unit in ([i] if task == "hidden" else range(UNITS, UNITS + 4)):
                        for g in groups_after(unit, 2):
                            q = g % NG
                            act.wait_ge(s_tr, g + 1)
                            if g >= HT_RING:
                                act.wait_ge(s_dn, g - HT_RING + 1)
                            full = sum(1 for f in range(*GROUPS[q]) if f < FB - 1) * P
                            last = act.copy(hT[:, g % HT_RING, 0:full], psM[:, 0:full])
                            if q == NG - 1:
                                last = act.copy(hT[0:LASTF, g % HT_RING, full:full + P], psM[0:LASTF, full:full + P])
                            last.then_inc(s_ht, 1)

        @block.vector
        def _(dve):
            links = [0]

            def link(ins):
                links[0] += 1
                ins.then_inc(s_chain, 1)
                dve.wait_ge(s_chain, links[0])

            def mul(unit):
                t, j = divmod(unit, NU)
                b, lh = divmod(t, LH)
                if unit == 0:
                    dve.wait_ge(s_wlo, NSPLIT)
                if j == 0 and t >= 2:
                    dve.wait_ge(s_tr, NG * (t - 1))
                dve.wait_ge(s_ag, unit + 1)
                dst = hcat[:, t % 2, j * FF:(j + 1) * FF]
                up = psU[:, unit % 2, FF:2 * FF]
                if j < 2:
                    last = dve.tensor_tensor(dst, ag[:, unit % 2, :], up, ALU.mult)
                else:
                    if j == 2:
                        dve.wait_ge(s_w, t + 1)
                    last = dve.scalar_tensor_tensor(dst, up, wtok[:, b % 2, lh, j - 2:j - 1], ag[:, unit % 2, :],
                                                    ALU.mult, ALU.mult)
                last.then_inc(s_mul, 1)

            def after_last():
                dve.wait_ge(s_chain, links[0])

            def chained(ins):
                links[0] += 1
                ins.then_inc(s_chain, 1)

            for task, i in order:
                if task == "load":
                    dve.memset(zeros[:, :], 0.0).then_inc(s_blank, 1)
                    dve.memset(psA.rearrange("p r (c l) -> p r c l", l=P)[:, :, :, 0:1], 0.0).then_inc(s_zero, 1)
                    dve.memset(minus_half[:, :], -0.5).then_inc(s_mh, 1)
                    dve.wait_ge(d_par, 16)
                    dve.tensor_scalar(cwh[:, :], par[:, PC_CONVW:PC_DTB], 0.5, None, ALU.mult).then_inc(s_half, 1)
                    dve.wait_ge(s_gt, 1)
                    dve.tensor_scalar(gates[:, :], gtanh[:, :], 0.5, None, ALU.mult).then_inc(s_gates, 1)
                    dve.wait_ge(s_aexp, 1)
                    dve.tensor_scalar(aneg[:, :], aexp[:, :], -1.0, None, ALU.mult).then_inc(s_aneg, 1)
                elif task in ("tap0", "tap1", "tap2"):
                    k = int(task[-1])
                    back = DC - 1 - k
                    dve.wait_ge(s_xh, (EH + 1) * (i + 1))
                    if i == 0:
                        dve.wait_ge(s_half, 1)
                    for h in range(EH):
                        if k >= 1:
                            dve.wait_ge(s_tap, EH * ((DC - 1) * i + k - 1) + h + 1)
                        dve.scalar_tensor_tensor(xh[:, h, back:L], xraw[:, h, 0:L - back],
                                                 Wh[:, h, k:k + 1], xh[:, h, back:L],
                                                 ALU.mult, ALU.add).then_inc(s_tap, 1)
                elif task == "silu_u":
                    dve.wait_ge(s_tu, i + 1)
                    if i >= 2:
                        dve.wait_ge(s_uD, LH * (i - 1))
                        dve.wait_ge(s_du, i - 1)
                    dve.scalar_tensor_tensor(u[:, i % 2], tu[:, :, :], 1.0, xh[:, :, :], ALU.add,
                                             ALU.mult).then_inc(s_u, 1)
                elif task[:-1] == "split":
                    m1, m2 = 2 * 2 * DS, 2 * DS
                    if task == "split0":
                        dve.wait_ge(s_hi, i + 1)
                        dve.tensor_tensor(rest1[:, :], xdbl[0:m1, :], parts[0:m1, i % 2, :], ALU.subtract).then_inc(s_rest, 1)
                    elif task == "split1":
                        dve.wait_ge(s_rest, i + 1)
                        chained(dve.tensor_copy(parts[0:m1, i % 2, :], rest1[:, :]))
                    elif task == "split2":
                        after_last()
                        chained(dve.tensor_tensor(rest2[:, :], rest1[0:m2, :], parts[0:m2, i % 2, :], ALU.subtract))
                    else:
                        after_last()
                        dve.tensor_copy(parts[0:m2, i % 2, :], rest2[:, :]).then_inc(s_parts, 1)
                elif task == "log_1":
                    dve.wait_ge(s_exp, i + 1)
                    chained(dve.tensor_scalar(dy[:, :, :], dexp[:, :, :], 1.0, None, ALU.add))
                elif task == "log_2":
                    after_last()
                    dve.scalar_tensor_tensor(dnc[:, :, :], dy[:, :, :], -1.0, dexp[:, :, :], ALU.add,
                                             ALU.subtract).then_inc(s_dnc, 1)
                elif task[:-1] == "delta" and i <= 1:
                    finish_delta(dve, task, i)
                elif task == "scan":
                    b, s0, l0, l1 = step_range(i)
                    dve.wait_ge(s_dA, i + 1)
                    dve.wait_ge(s_dbu, i + 1)
                    if i >= 2:
                        dve.wait_ge(s_prod, i - 1)
                    if l0:
                        dve.wait_ge(s_fix, fixes(i))
                    dve.tensor_tensor_scan(hs[:, i % 2], psA[:, i % DA_RING], dbu[:, i % DBU_RING], 0.0,
                                           ALU.mult, ALU.add).then_inc(s_scan, 1)
                elif task == "carry_in":
                    dve.wait_ge(s_dbu, i + 1)
                    dve.wait_ge(s_carry, fixes(i))
                    heads = dbu[:, i % DBU_RING].rearrange("p (c l) -> p c l", l=P)[:, :, 0]
                    dve.tensor_tensor(heads, heads, carry[:, i % HALF, :], ALU.add).then_inc(s_fix, 1)
                elif task == "edge_in":
                    dve.wait_ge(s_delta, i + 1)
                    if i == 0:
                        dve.wait_ge(s_aneg, 1)
                    else:
                        dve.wait_ge(s_edge_dA, i)
                    for h in range(EH):
                        last = dve.tensor_scalar(eraw[:, h, :], aneg[:, h * DS:(h + 1) * DS], delta[:, i % 2, h, P:P + 1],
                                                 None, ALU.mult)
                    last.then_inc(s_edge, 1)
                elif task == "prod":
                    b, s0, l0, l1 = step_range(i)
                    dve.wait_ge(s_scan, i + 1)
                    if l0 == 0:
                        if s0 == 0:
                            dve.wait_ge(s_edge_dA, b + 1)
                        dve.tensor_tensor(carry[:, s0 // LH, :].rearrange("p (s h) -> p s h", s=LH),
                                          tile(hs[:, i % 2])[:, :, :, P - 1],
                                          edge.rearrange("p h n -> p n h")[:, s0:s0 + LH, :], ALU.mult).then_inc(s_carry, 1)
                    dve.wait_ge(s_cps, i + 1)
                    if i >= PROD_RING:
                        dve.wait_ge(*added(i - PROD_RING))
                    c = psC[:, i % 2, 0:NS * (l1 - l0)].rearrange("p (s l) -> p s l", s=NS)
                    dve.tensor_tensor(tile(prod[:, i % PROD_RING]), tile(hs[:, i % 2]),
                                      c.unsqueeze(2).broadcast_to([P, NS, EH, l1 - l0]), ALU.mult).then_inc(s_prod, 1)
                elif task == "z_stats":
                    if i == 0:
                        dve.wait_ge(d_x0, 16)
                    if i == 1:
                        dve.wait_ge(d_x, 16 * (B - 1))
                    for h in range(LH):
                        dve.bn_stats(zst[:, i * LH + h, :], x_sb[:, i, h, :]).then_inc(s_zst, 1)
                    dve.wait_ge(s_zst, LH * (i + 1))
                    for h in range(LH):
                        dve.bn_aggr(zmv[:, i * LH + h, :], zst[:, i * LH + h, :]).then_inc(s_zmv, 1)
                elif task == "z_norm":
                    dve.wait_ge(s_zrs, i + 1)
                    dve.wait_ge(s_zmv, LH * (i + 1))
                    if i >= 1:
                        dve.wait_ge(s_zt, i)
                    for h in range(LH):
                        c = i * LH + h
                        dve.tensor_scalar(zn[:, h, :], x_sb[:, i, h, :], zmv[:, c, 0:1], zrs[:, c:c + 1],
                                          ALU.subtract, ALU.mult).then_inc(s_zn, 1)
                elif task == "z_gate":
                    dve.wait_ge(s_zt, i + 1)
                    dve.scalar_tensor_tensor(sz[:, :, :], zt[:, :, :], 1.0, zn[:, :, :], ALU.add,
                                             ALU.mult).then_inc(s_sz, 1)
                elif task == "gate_y":
                    b, h = divmod(i, LH)
                    l0, l1 = h * P, (h + 1) * P
                    dve.wait_ge(*added(part_end(i) - 1))
                    if i == 0:
                        total = psD[:, 0, :].rearrange("p (h l) -> p h l", h=EH)
                    else:
                        even, odd = (tile(acc[:, i % 2])[:, j] for j in range(LH))
                        dve.tensor_tensor(ysum[:, :, :], even, odd, ALU.add).then_inc(s_y2, 1)
                        dve.wait_ge(s_y2, i)
                        total = ysum[:, :, :]
                    dve.wait_ge(s_uD, i + 1)
                    dve.tensor_tensor(ysum[:, :, :], total, uD[:, :, :], ALU.add).then_inc(s_ys, 1)
                    dve.wait_ge(s_ys, i + 1)
                    dve.wait_ge(s_sz, b + 1)
                    if i >= 1:
                        dve.wait_ge(s_yT, i)
                    dve.tensor_tensor(yg[:, :, l0:l1], ysum[:, :, :], sz[:, :, l0:l1], ALU.mult).then_inc(s_yg, 1)
                elif task == "residual":
                    b, h = divmod(i, LH)
                    r = slice(h, h + 1)
                    dve.wait_ge(s_yT, i + 1)
                    if i == 0:
                        dve.wait_ge(s_gates, 1)
                    dve.scalar_tensor_tensor(x2[:, b, r], psM.rearrange("p (h d) -> p h d", h=LH)[:, r], gates[:, 0:1],
                                             x_sb[:, b, r], ALU.mult, ALU.add).then_inc(s_x2, 1)
                elif task == "stats":
                    b, h = divmod(i, LH)
                    dve.wait_ge(s_x2, i + 1)
                    dve.bn_stats(st2[:, h, :], x2[:, b, h, :]).then_inc(s_st2, 1)
                elif task == "variance":
                    b, h = divmod(i, LH)
                    dve.wait_ge(s_st2, i + 1)
                    if i >= 1:
                        dve.wait_ge(s_rs2, i)
                    dve.bn_aggr(mv2[:, h, :], st2[:, h, :]).then_inc(s_mv2, 1)
                elif task == "norm":
                    b, h = divmod(i, LH)
                    dve.wait_ge(s_rs2, i + 1)
                    dve.wait_ge(s_mv2, i + 1)
                    if i >= 1:
                        dve.wait_ge(s_hT2, i)
                    dve.tensor_scalar(hn[:, h, :], x2[:, b, h, :], mv2[:, h, 0:1], rs2[:, h:h + 1],
                                      ALU.subtract, ALU.mult).then_inc(s_hn, 1)
                elif task[:-1] == "route":
                    b, h = divmod(i, LH)
                    r = slice(h, h + 1)
                    c = slice(h * NE, (h + 1) * NE)
                    if task == "route0":
                        dve.wait_ge(s_rex, i + 1)
                        chained(dve.tensor_scalar(rs1[:, c], rex[:, c], 1.0, None, ALU.add))
                        continue
                    after_last()
                    if task == "route1":
                        last = dve.reciprocal(score[:, c], rs1[:, c])
                    elif task == "route2":
                        last = dve.max(top[:, h, :], score[:, h * NE:(h + 1) * NE])
                    elif task == "route3":
                        last = dve.max_index(topi[:, h, :], top[:, h, :], score[:, h * NE:(h + 1) * NE])
                    elif task == "route4":
                        dve.tensor_copy(topf[:, r, :], topi[:, r, 0:2])
                        link(dve.scalar_tensor_tensor(den[:, r], top[:, r, 0], 1e-20, top[:, r, 1], ALU.add, ALU.add))
                        last = dve.reciprocal(rden[:, r], den[:, r])
                    elif task == "route5":
                        last = dve.scalar_tensor_tensor(topw[:, r, :], top[:, r, 0:2], SCALE,
                                                        rden[:, r].unsqueeze(2).broadcast_to([P, 1, 2]),
                                                        ALU.mult, ALU.mult)
                    else:
                        for k in range(2):
                            last = dve.tensor_scalar(pick[:, h, k, :], par[:, PC_IOTA:PC_IOTA + NE],
                                                     topf[:, h, k:k + 1], topw[:, h, k:k + 1], ALU.is_equal, ALU.mult)
                        link(last)
                        dve.tensor_tensor(wtok[:, b % 2, r], pick[:, r, 0, :], pick[:, r, 1, :], ALU.add).then_inc(s_w, 1)
                        continue
                    chained(last)
                elif task == "mul":
                    mul(i)
                elif task == "gate":
                    dve.wait_ge(s_tanh, i + 1)
                    dve.scalar_tensor_tensor(ag[:, i % 2, :], tg[:, i % 2, :], 1.0, psU[:, i % 2, 0:FF], ALU.add,
                                             ALU.mult).then_inc(s_ag, 1)
                if task in ("hidden", "flush"):
                    for unit in ([i] if task == "hidden" else range(UNITS, UNITS + 4)):
                        for g in groups_after(unit, 4):
                            t, q = divmod(g, NG)
                            if q == NG - 1:
                                b, lh = divmod(t, LH)
                                dve.wait_ge(s_dn, g + 1)
                                if t >= 2:
                                    dve.wait_ge(d_out[t % 2], 16 * (t // 2))
                                dve.scalar_tensor_tensor(outb[:, t % 2, :], psD[:, 0, :], gates[:, 1:2],
                                                         x2[:, b, lh, :], ALU.mult, ALU.add).then_inc(s_fin, 1)

        @block.gpsimd
        def _(pool):
            def times_b(m):
                b, s0, l0, l1 = step_range(m)
                if m % DS == 0:
                    pool.wait_ge(s_du, b + 1)
                if m < HALF and s0 < PE_STATES and s0 % 4 == 0:
                    pool.wait_ge(s_bb, s0 // 4 + 1)
                if m < HALF and s0 == PE_STATES:
                    pool.wait_ge(d_bb, 32)
                if b >= 1 and m % DS == 0:
                    pool.wait_ge(d_bb, 16 * (b + 2))
                if m >= DBU_RING:
                    pool.wait_ge(s_scan, m - DBU_RING + 1)
                shape = [P, NS, EH, l1 - l0]
                pool.tensor_tensor(tile(dbu[:, m % DBU_RING]),
                                   du[:, b % 2, :, l0:l1].unsqueeze(1).broadcast_to(shape),
                                   bb[:, b % 2, s0:s0 + NS, l0:l1].unsqueeze(2).broadcast_to(shape),
                                   ALU.mult).then_inc(s_dbu, 1)

            for task, i in order:
                if task == "first":
                    times_b(0)
                elif task == "scan":
                    if i + 1 < STEPS:
                        times_b(i + 1)
                elif task[:-1] == "delta" and i >= 2:
                    finish_delta(pool, task, i)
                elif task == "prod" and not on_pe(i) and i % HALF:
                    p = i // HALF
                    pool.wait_ge(s_prod, i + 1)
                    if i % HALF == 1:
                        if p >= 3:
                            pool.wait_ge(s_ys, p - 1)
                        before = prod[:, (i - 1) % PROD_RING]
                    else:
                        pool.wait_ge(*added(i - 1))
                        before = acc[:, p % 2]
                    pool.tensor_tensor(acc[:, p % 2], before, prod[:, i % PROD_RING], ALU.add).then_inc(s_add, 1)
                elif task == "z_stats":
                    pool.wait_ge(s_zmv, LH * (i + 1))
                    if i == 0:
                        pool.wait_ge(s_mh, 1)
                    c = slice(i * LH, (i + 1) * LH)
                    pool.tensor_scalar(zve[:, c], zmv[:, c, 1], EPS, None, ALU.add).then_inc(s_zve, 1)
                    pool.wait_ge(s_zve, i + 1)
                    pool.tensor_tensor(zrs[:, c], zve[:, c], minus_half[:, c], ALU.pow).then_inc(s_zrs, 1)
                elif task == "features_lo":
                    b, h = divmod(i, LH)
                    pool.wait_ge(s_hnhi, i + 1)
                    pool.tensor_tensor(hnlo[:, i % 2], hnT[:, b % 2, :, h * P:(h + 1) * P], hnhi[:, i % 2],
                                       ALU.subtract).then_inc(s_hnlo, 1)
                elif task == "weights_lo":
                    pool.wait_ge(s_whi, i + 1)
                    pool.tensor_tensor(wlo[:, i], staged[:, i], whi[:, i], ALU.subtract).then_inc(s_wlo, 1)
                elif task == "variance":
                    b, h = divmod(i, LH)
                    r = slice(h, h + 1)
                    pool.wait_ge(s_mv2, i + 1)
                    if i >= 1:
                        pool.wait_ge(s_hn, i)
                    pool.tensor_scalar(ve2[:, r], mv2[:, r, 1], EPS, None, ALU.add).then_inc(s_ve2, 1)
                    pool.wait_ge(s_ve2, i + 1)
                    pool.tensor_tensor(rs2[:, r], ve2[:, r], minus_half[:, 0:1], ALU.pow).then_inc(s_rs2, 1)


def kernel(**inputs):
    import concourse.bacc as bacc
    import ml_dtypes
    from concourse.bass_utils import run_bass_kernel_spmd

    a = {k: np.asarray(v) for k, v in inputs.items()}

    def halves(w):
        return w.reshape(w.shape[0], -1, P).transpose(2, 1, 0)

    def channels(w):
        return w.reshape(EH, P, -1).transpose(1, 0, 2).reshape(P, -1)

    params = np.concatenate([
        channels(a["L0_xattn_conv_w"]), channels(a["L0_xattn_conv_b"]), channels(a["L0_xattn_dt_proj_b"]),
        channels(a["L0_xattn_D"]), channels(a["L0_xattn_A_log"]),
        np.broadcast_to(a["g_xattn"].reshape(1, 1), (P, 1)), np.broadcast_to(a["g_ffn"].reshape(1, 1), (P, 1)),
        np.broadcast_to(np.arange(NE, dtype=np.float32), (P, NE))], axis=1)
    wx = a["L0_xattn_x_proj_w"]
    gate = np.concatenate([a["L0_ffn_shared_wg"].reshape(2, FF, D), a["L0_ffn_exp_wg"]])
    up = np.concatenate([a["L0_ffn_shared_wu"].reshape(2, FF, D), a["L0_ffn_exp_wu"]])
    both = np.concatenate([gate, up], axis=1)
    rows = np.arange(XROWS) % (2 * DS)
    arrays = {
        "ctxT": a["ctx_1024"].transpose(2, 0, 1),
        "x": a["x"],
        "params": params,
        "w_in": a["L0_xattn_in_proj_w"].T,
        "w_x": halves(np.concatenate([wx[DR:], wx[DR:], wx[DR:], wx[:DR]])),
        "w_dt": a["L0_xattn_dt_proj_w"].T,
        "w_gate": halves(a["L0_ffn_gate_w"]),
        "w_up": both.reshape(NU, 2 * FF, KT, P).transpose(3, 0, 2, 1),
        "w_down": np.concatenate([a["L0_ffn_shared_wd"].T, a["L0_ffn_exp_wd"].transpose(0, 2, 1).reshape(NE * FF, D)]),
        "ident": np.eye(P, dtype=np.float32),
        "sel": np.broadcast_to((rows[:, None] == np.arange(2 * DS))[:, :, None],
                               (XROWS, 2 * DS, P)).astype(ml_dtypes.bfloat16),
    }
    arrays = {f"in_{k}": np.ascontiguousarray(v) for k, v in arrays.items()}
    nc = bacc.Bacc("TRN2", target_bir_lowering=False, num_devices=1)
    args = [nc.dram_tensor(k, v.shape, mybir.dt.from_np(v.dtype), kind="ExternalInput").ap() for k, v in arrays.items()]
    out = nc.dram_tensor("out_0", (B, L, D), F32, kind="ExternalOutput").ap()
    mixer(nc, *args, out)
    return run_bass_kernel_spmd(nc, [arrays], core_ids=[0]).results[0]["out_0"]
```
